# Optimizing a Trainium2 kernel written in Bass

```python
import numpy as np
import jax
import jax.numpy as jnp

def _softmax(x, axis=-1):
    return jax.nn.softmax(x, axis=axis)
def _gelu(x):
    return jax.nn.gelu(x, approximate=True)
def _silu(x):
    return jax.nn.silu(x)
def _sigmoid(x):
    return jax.nn.sigmoid(x)
def _layernorm(x, axis=-1, eps=1e-5):
    m = jnp.mean(x, axis=axis, keepdims=True)
    v = jnp.var(x, axis=axis, keepdims=True)
    return (x - m) / jnp.sqrt(v + eps)
def _scatter_add(tgt, idx, src, axis=0):
    return tgt.at[idx].add(src)
def _segment_sum(src, seg, n):
    return jax.ops.segment_sum(src, seg, n)

kernel_name = 'mk_conv_preact_d2_conv_nchw512_33f758'

def setup_inputs(seed: int = 0):
    np.random.seed(seed)
    _w = jnp.asarray
    def _rec_inputs():
        import jax
        import jax.numpy as jnp
        _gk = jax.random.key(seed)
        x = -0.000125 + 0.9999 * jax.random.normal(jax.random.fold_in(_gk, 1), (16, 512, 64, 64), jnp.float32)
        return x
    x = _rec_inputs()
    def _L0_conv_setup():
        import jax, jax.numpy as jnp
        import numpy as np
        KERNEL_SIZE = 5
        EPS = 1e-06

        def spatial_descriptor(x, k):
            b, c, h, w = x.shape
            p = k // 2
            xp = jnp.pad(x, ((0, 0), (0, 0), (p, p), (p, p)))
            corrs = [jnp.sum(x * jax.lax.dynamic_slice(xp, (0, 0, di, dj), (b, c, h, w)), axis=1) for di in range(k) for dj in range(k)]
            return jnp.stack(corrs, axis=1)
        key = jax.random.key(seed)
        k1, k2 = jax.random.split(key)
        b, c, h, w = (16, 512, 64, 64)
        hidden = 512
        input_dim = c + KERNEL_SIZE * KERNEL_SIZE
        x = jax.random.normal(k1, (b, c, h, w), dtype=jnp.float32)
        W = jax.random.normal(k2, (hidden, input_dim), dtype=jnp.float32) * (1.0 / np.sqrt(input_dim))
        bias = jnp.zeros((hidden,), dtype=jnp.float32)
        return {'x': x, 'W': W, 'bias': bias}
    _L0_conv_all = _L0_conv_setup()
    _L0_conv_in = {k: v for k, v in _L0_conv_all.items() if k in ('W', 'bias', )}
    del _L0_conv_all

    def _L1_conv_setup():
        import jax, jax.numpy as jnp
        import numpy as np
        KERNELS = (1, 3, 5, 7, 9, 11, 13)

        def _maxpool_same(x, k):
            if k == 1:
                return x
            return jax.lax.reduce_window(x, -jnp.inf, jax.lax.max, window_dimensions=(1, 1, k, k), window_strides=(1, 1, 1, 1), padding='SAME')
        key = jax.random.key(seed)
        k_x, k_w1, k_b1, k_w2, k_b2 = jax.random.split(key, 5)
        b, c, h, w = (8, 512, 64, 64)
        c16 = c // 16
        x = jax.random.normal(k_x, (b, c, h, w), dtype=jnp.float32)
        w1 = jax.random.normal(k_w1, (c16, c), dtype=jnp.float32) * (1.0 / np.sqrt(c))
        b1 = jax.random.normal(k_b1, (c16,), dtype=jnp.float32) * 0.1
        w2 = jax.random.normal(k_w2, (c, c16), dtype=jnp.float32) * (1.0 / np.sqrt(c16))
        b2 = jax.random.uniform(k_b2, (c,), dtype=jnp.float32, minval=0.0, maxval=6.0)
        return {'x': x, 'w1': w1, 'b1': b1, 'w2': w2, 'b2': b2}
    _L1_conv_all = _L1_conv_setup()
    _L1_conv_in = {k: v for k, v in _L1_conv_all.items() if k in ('w1', 'b1', 'w2', 'b2', )}
    del _L1_conv_all

    return {
        "x": x,
        "L0_conv_W": _L0_conv_in["W"],
        "L0_conv_bias": _L0_conv_in["bias"],
        "L1_conv_w1": _L1_conv_in["w1"],
        "L1_conv_b1": _L1_conv_in["b1"],
        "L1_conv_w2": _L1_conv_in["w2"],
        "L1_conv_b2": _L1_conv_in["b2"],
    }

def reference(x, L0_conv_W, L0_conv_bias, L1_conv_w1, L1_conv_b1, L1_conv_w2, L1_conv_b2):
    import jax
    import jax.numpy as jnp
    def _L0_conv_ref(x, W, bias):
        import jax, jax.numpy as jnp
        import numpy as np
        KERNEL_SIZE = 5
        EPS = 1e-06

        def spatial_descriptor(x, k):
            b, c, h, w = x.shape
            p = k // 2
            xp = jnp.pad(x, ((0, 0), (0, 0), (p, p), (p, p)))
            corrs = [jnp.sum(x * jax.lax.dynamic_slice(xp, (0, 0, di, dj), (b, c, h, w)), axis=1) for di in range(k) for dj in range(k)]
            return jnp.stack(corrs, axis=1)
        k = KERNEL_SIZE
        gs = spatial_descriptor(x, k)
        norm = jnp.sqrt(jnp.sum(gs * gs, axis=1, keepdims=True) + EPS)
        gs = gs / norm
        feat = jnp.concatenate([x, gs], axis=1)
        out = jnp.einsum('bchw,oc->bohw', feat, W) + bias[None, :, None, None]
        return jax.nn.relu(out)

    def _L1_conv_ref(x, w1, b1, w2, b2):
        import jax, jax.numpy as jnp
        import numpy as np
        KERNELS = (1, 3, 5, 7, 9, 11, 13)

        def _maxpool_same(x, k):
            if k == 1:
                return x
            return jax.lax.reduce_window(x, -jnp.inf, jax.lax.max, window_dimensions=(1, 1, k, k), window_strides=(1, 1, 1, 1), padding='SAME')
        b, c, h, w = x.shape
        n_k = len(KERNELS)
        gap = jnp.mean(x, axis=(2, 3))
        hmid = jax.nn.relu(jnp.einsum('bc,ec->be', gap, w1) + b1)
        score = jnp.einsum('be,ce->bc', hmid, w2) + b2
        s = jax.nn.relu(score)
        q_s = jnp.clip(jnp.floor(jax.lax.stop_gradient(s)), 0, n_k - 2).astype(jnp.int32)
        q_b = q_s + 1
        pools = jnp.stack([_maxpool_same(x, k) for k in KERNELS], axis=2)
        s_out = jnp.take_along_axis(pools, q_s[:, :, None, None, None], axis=2)[:, :, 0]
        b_out = jnp.take_along_axis(pools, q_b[:, :, None, None, None], axis=2)[:, :, 0]
        frac_b = (s - q_s.astype(s.dtype))[:, :, None, None]
        frac_s = (q_b.astype(s.dtype) - s)[:, :, None, None]
        return frac_b * b_out + frac_s * s_out + x

    def _gn(v, G=32, eps=1e-5):
        B_, C_, H_, W_ = v.shape
        g = v.reshape(B_, G, C_ // G, H_, W_)
        m = jnp.mean(g, axis=(2, 3, 4), keepdims=True)
        s = jnp.var(g, axis=(2, 3, 4), keepdims=True)
        return ((g - m) / jnp.sqrt(s + eps)).reshape(v.shape)

    def _ln_c(v, eps=1e-6):
        m = jnp.mean(v, axis=1, keepdims=True)
        s = jnp.var(v, axis=1, keepdims=True)
        return (v - m) / jnp.sqrt(s + eps)

    def _ln_t(v, eps=1e-5):
        m = jnp.mean(v, axis=-1, keepdims=True)
        s = jnp.var(v, axis=-1, keepdims=True)
        return (v - m) / jnp.sqrt(s + eps)

    def _to_tokens(v):
        B_, C_, H_, W_ = v.shape
        return v.reshape(B_, C_, H_ * W_).transpose(0, 2, 1)
    def _from_tokens(t, like):
        B_, C_, H_, W_ = like.shape
        return t.transpose(0, 2, 1).reshape(B_, C_, H_, W_)

    x = x + _L0_conv_ref(_gn(x), L0_conv_W, L0_conv_bias)
    x = x + _L1_conv_ref(_gn(x), L1_conv_w1, L1_conv_b1, L1_conv_w2, L1_conv_b2)
    return x


_drawn_inputs = setup_inputs


def setup_inputs(seed=0):
    import zlib

    import numpy as np

    out = dict(_drawn_inputs(seed))
    spreads = {'L0_conv_bias': (0.0, 0.1)}
    factors = {'L1_conv_w1': 7.04, 'L1_conv_b1': 3.854}
    for name, (base, spread) in spreads.items():
        noise = np.random.default_rng([zlib.crc32(name.encode()), seed]).standard_normal(out[name].shape)
        drawn = base * np.exp(spread * noise) if base else spread * noise
        out[name] = jnp.asarray(drawn.astype(out[name].dtype))
    for name, factor in factors.items():
        out[name] = (out[name] * factor).astype(out[name].dtype)
    return out
```

```python
import numpy as np
from contextlib import ExitStack

import concourse.bass as bass
from concourse import mybir

P = 128
C, H, W = 512, 64, 64
PIX = H * W
CT = C // P
ROWS = 8
CH = H // ROWS
CW = ROWS * W
NB = H // 2
PAIRS = ROWS // 2
KS = 5
D = KS * KS
CG = 16
HID = 32
NCLS = 6
SC = 64.0
EPS = 1e-5
EPS_D = 1e-6
RING = 4
LOWEST = -3.4028234663852886e38
PADC = 6
REC = 8
BUFS = 4
REP = 3 * 32


def const_arrays():
    p = np.arange(P)
    r, w = p // W, p % W
    q = np.arange(2 * W)
    band = (np.abs(w[:, None] - (q % W)[None, :]) <= KS // 2).astype(np.float32)
    pick = np.zeros((P, 3, 6 * KS), np.float32)
    for role in range(3):
        pick[p, role, (2 * (2 - role) + r) * KS + w % KS] = 1.0
    turn = np.zeros((P, 2, KS, REP), np.float32)
    for e in range(2):
        for k in range(KS):
            for di in range(-2, 3):
                for dj in range(-2, 3):
                    for rep in range(3):
                        turn[(di + 2 + e) * KS + (k + dj) % KS, e, k, 32 * rep + (di + 2) * KS + dj + 2] = 1.0
    ssum = np.zeros((P, REP), np.float32)
    ssum[:D] = 2.0 ** -12
    gavg = (p[:, None] // CG == p[None, :] // CG).astype(np.float32) / CG
    ident = np.eye(P, dtype=np.float32)
    before = (p[:, None] < p[None, :]).astype(np.float32)
    ones = np.ones((P, P), np.float32)
    return np.concatenate([band, pick.reshape(P, -1), turn.reshape(P, -1), ssum, gavg, ident, before, ones], axis=1)


CONST_W = 2 * W + 3 * 6 * KS + 2 * KS * REP + REP + 4 * P


def build(nc, x, wt, bias, w1t, b1, w2t, b2, consts, out):
    fp32, fp16, i32 = mybir.dt.float32, mybir.dt.float16, mybir.dt.int32
    ALU, ACT, AX = mybir.AluOpType, mybir.ActivationFunctionType, mybir.AxisListType
    B = x.shape[0]
    NC = B * CT
    NPL = NC * P
    NT = -(-(NC + NCLS - 1) // BUFS) * BUFS
    assert B >= 2
    nc.disable_value_cache = True

    x_v = x.rearrange("b (t p) h w -> b p t (h w)", p=P)
    out_rows = out.rearrange("b c h w -> (b c) (h w)")
    y_dram = nc.dram_tensor("y_planes", [NPL, PIX], fp32, kind="Internal").ap()
    y_v = y_dram.rearrange("(b t p) n -> b p t n", t=CT, p=P)
    rec_dram = nc.dram_tensor("plane_records", [NT * P, REC], fp32, kind="Internal").ap()

    ctx = ExitStack()
    with ctx:
        def sem(name):
            return ctx.enter_context(nc.semaphore(name))

        def sb(name, shape, dt):
            return ctx.enter_context(nc.sbuf_tensor(name, shape, dt))

        cst = sb("cst", [P, CONST_W], fp32)
        o = 0
        band = cst[:, o:o + 2 * W]; o += 2 * W
        pick = cst[:, o:o + 90].rearrange("p (r m) -> p r m", r=3); o += 90
        turn = cst[:, o:o + 2 * KS * REP].rearrange("p (e k m) -> p e k m", e=2, k=KS); o += 2 * KS * REP
        ssum = cst[:, o:o + REP]; o += REP
        gavg = cst[:, o:o + P]; o += P
        ident = cst[:, o:o + P]; o += P
        before = cst[:, o:o + P]; o += P
        ones = cst[:, o:o + P]; o += P
        bias_sb = sb("bias_sb", [P, CT], fp32)
        epsd = sb("epsd", [P, 1], fp32)
        epsg = sb("epsg", [P, 1], fp32)
        bnx = sb("bnx", [P, CT, CH, 6], fp32)
        bny = sb("bny", [P, CT, CH, 6], fp32)
        aggx = sb("aggx", [P, CT, 2], fp32)
        aggy = sb("aggy", [P, CT, 2], fp32)
        ymv = sb("ymv", [P, B * CT * 2], fp32)
        gm = sb("gm", [P, CT], fp32)
        gd = sb("gd", [P, CT], fp32)
        grs = sb("grs", [P, CT], fp32)
        gmean = sb("gmean", [P, CT], fp32)
        grstd = sb("grstd", [P, CT], fp32)

        ARENA = 50432
        arena = sb("arena", [P, ARENA], fp32)
        pos = [0]

        def take(n):
            pos[0] += n
            assert pos[0] <= ARENA
            return arena[:, pos[0] - n:pos[0]]

        take(2 * CT * PIX)
        gh = take(CT * RING * CW // 2).bitcast(fp16).rearrange("p (t n) -> p t n", t=CT)
        gl = take(CT * RING * CW // 2).bitcast(fp16).rearrange("p (t n) -> p t n", t=CT)
        sort_scratch = arena[:, 2 * CT * PIX:2 * CT * PIX + CT * RING * CW]
        g32 = take(2 * CW).rearrange("p (s n) -> p s n", s=2)
        bq = take(3 * 8 * P).rearrange("p (r n) -> p r n", r=3)
        frot = take(CW)
        sq = take(CW)
        fn = take(CW)
        tpair = take(CW).bitcast(fp16).rearrange("p (s n) -> p s n", s=2)
        relu = take(2 * CW).rearrange("p (s n) -> p s n", s=2)
        wh = take(CT * C // 2).bitcast(fp16).rearrange("p (t n) -> p t n", t=CT)
        wl = take(CT * C // 2).bitcast(fp16).rearrange("p (t n) -> p t n", t=CT)
        wd = take(C // 2).bitcast(fp16)
        stage_w = arena[:, CT * PIX:CT * PIX + CT * C].rearrange("p (t n) -> p t n", t=CT)
        stage_d = arena[:, CT * PIX + CT * C:CT * PIX + CT * C + C]
        stage_rec = arena[:, CT * PIX + (CT + 1) * C:CT * PIX + (CT + 1) * C + NT * REC]

        bq_off = 2 * CT * PIX + CT * RING * CW + 2 * CW

        def xs_quarter(par, q):
            return arena[:, bass.ds(par * (CT * PIX), CT * PIX)]\
                .rearrange("p (t n) -> p t n", t=CT)[:, :, q * (PIX // 4):(q + 1) * (PIX // 4)]

        pos[0] = 2 * CT * PIX
        v = lambda n: take(n)
        w1_sb = v(CT * HID).rearrange("p (t e) -> p t e", t=CT)
        w2_sb = v(C)
        b1_sb = v(1)
        b2_sb = v(CT)
        sm, sd, sa, sr, scc, sgap = (v(NC) for _ in range(6))
        score, cls, fs, fb, tmp = (v(NC) for _ in range(5))
        hid = v(B)
        onehot = v(NCLS * NC)
        incl = v(NCLS * NC)
        rank = v(NCLS * NC)
        zeros = v(NC)
        tiles, tincl, tbase, tb128 = (v(NCLS) for _ in range(4))
        slot_f = v(NC)
        slot_i = v(NC).bitcast(i32)
        tnum_i = v(NT).bitcast(i32)
        tnum = v(NT)
        tcls = v(NT)
        recs = v(NC * REC).rearrange("p (n e) -> p n e", e=REC)
        assert pos[0] <= bq_off
        pos[0] = 0
        bufs = v(BUFS * PIX).rearrange("p (b n) -> p b n", b=BUFS)
        WP = W + 2 * PADC
        ypad_f = v(H * WP)
        ypad = ypad_f.rearrange("p (h w) -> p h w", w=WP)
        hbuf_f = v((H + 2 * PADC) * W)
        hbuf = hbuf_f.rearrange("p (h w) -> p h w", w=W)
        small_f = v(2 * H * (W + 2))
        small = small_f.rearrange("p (s h w) -> p s h w", s=2, h=H)
        big = v(2 * PIX).rearrange("p (s n) -> p s n", s=2)
        half_m, half_w = v(36 * W), v(36 * W)
        rec_sb = v(NT * REC).rearrange("p (t e) -> p t e", e=REC)
        diag = v(2 * 3 * P).rearrange("p (s k n) -> p s k n", s=2, k=3)
        cls_i = v(NT).bitcast(i32)
        idx = v(BUFS).bitcast(i32)
        const_t = v(2)

        psum = ctx.enter_context(nc.psum_tensor("psum", [P, 8, 512], fp32))
        GRAM0, BANK_A, BANK_F = 4, 6, 7

        s_const = sem("s_const")
        s_stage = sem("s_stage")
        s_wd_in = sem("s_wd_in")
        s_pad = sem("s_pad")
        s_wsplit = sem("s_wsplit")
        x_loaded = [sem(f"x_loaded{q}") for q in range(4)]
        y_stored = [sem(f"y_stored{q}") for q in range(4)]
        s_xagg = sem("s_xagg")
        s_gavg = sem("s_gavg")
        s_gsq = sem("s_gsq")
        s_vchain = sem("s_vchain")
        s_g32 = sem("s_g32")
        s_gh = sem("s_gh")
        s_gl = sem("s_gl")
        s_chunk_used = sem("s_chunk_used")
        s_gram = sem("s_gram")
        s_masked = sem("s_masked")
        s_pick = sem("s_pick")
        s_frot = sem("s_frot")
        s_turn = sem("s_turn")
        s_sq = sem("s_sq")
        s_norm = sem("s_norm")
        s_root = sem("s_root")
        s_rinv = sem("s_rinv")
        s_fn = sem("s_fn")
        s_th = sem("s_th")
        s_t = sem("s_t")
        s_conv = sem("s_conv")
        s_relu = sem("s_relu")
        s_added = sem("s_added")
        s_y = sem("s_y")
        s_ymv = sem("s_ymv")
        s_yagg = sem("s_yagg")
        s_newton = sem("s_newton")
        s_issue = sem("s_issue")
        s_carry = sem("s_carry")
        s_w12 = sem("s_w12")
        s_link = sem("s_link")
        s_sstat = sem("s_sstat")
        s_smm = sem("s_smm")
        s_sroot = sem("s_sroot")
        s_iota = sem("s_iota")
        s_sorted = sem("s_sorted")
        s_scattered = sem("s_scattered")
        s_rec = sem("s_rec")
        s_pads = sem("s_pads")
        s_idx = sem("s_idx")
        gathered = [sem(f"gathered{b}") for b in range(BUFS)]
        written = [sem(f"written{b}") for b in range(BUFS)]
        s_ypad = sem("s_ypad")
        s_rows = sem("s_rows")
        s_own = sem("s_own")
        s_pool = sem("s_pool")
        s_diag = sem("s_diag")
        s_mix = sem("s_mix")
        s_res = sem("s_res")

        block = ctx.enter_context(nc.Block())

        STATS_CHAIN = 8

        def xs(ct, lo, n, par):
            return arena[:, bass.ds(par * (CT * PIX) + (ct * PIX + lo), n)]

        def gram_parts(t):
            lo, hi = max(2 * t - 2, 0), min(2 * t + 4, H)
            parts, row = [], lo
            while row < hi:
                slot_end = (row // (RING * ROWS) + 1) * RING * ROWS
                end = min(hi, slot_end)
                parts.append(((row - (2 * t - 2)) * W, (row % (RING * ROWS)) * W, (end - row) * W))
                row = end
            return parts

        def mask_runs(t):
            roles = [r for r in range(3) if 0 <= t - 1 + r < NB]
            runs = [[roles[0]]]
            for r in roles[1:]:
                if (t - 1 + r) % 8 == 0:
                    runs.append([])
                runs[-1].append(r)
            return [r for r in runs if r]

        def gram_blocks(c):
            first = 0 if c == 0 else PAIRS * c + 1
            return list(range(first, min(PAIRS * c + PAIRS + 1, NB)))

        @block.sync
        def _(sp):
            sp.dma_start(cst[:, :], consts[:, :]).then_inc(s_const, 16)
            sp.dma_start(bias_sb[:, :], bias.rearrange("(t p) -> p t", p=P),
                         allow_slow_non_contiguous=True).then_inc(s_const, 16)
            sp.dma_start(stage_w, wt[0:C, :].rearrange("(t p) n -> p t n", p=P)).then_inc(s_const, 16)
            for q in range(4):
                sp.dma_start(xs_quarter(0, q), x_v[0, :, :, q * 1024:(q + 1) * 1024]).then_inc(x_loaded[q], 16)
            sp.wait_ge(s_stage, 3)
            for rep in range(3):
                sp.dma_start(stage_d[32 * rep:32 * rep + D, :], wt[C:C + D, :]).then_inc(s_wd_in, 16)
            sp.dma_start(rec_dram.rearrange("(t p) e -> p t e", p=P),
                         stage_rec.rearrange("p (t e) -> p t e", e=REC)).then_inc(s_pad, 16)

            sp.wait_ge(s_wsplit, 5)
            sp.wait_ge(s_pad, 16)
            for q in range(4):
                sp.dma_start(xs_quarter(1, q), x_v[1, :, :, q * 1024:(q + 1) * 1024]).then_inc(x_loaded[q], 16)

            def quarters(i, load_next):
                for q in range(4):
                    sp.wait_ge(s_y, i * (CH * CT) + (q + 1) * 2 * CT)
                    sp.dma_start(y_v[bass.ds(i, 1), :, :, q * 1024:(q + 1) * 1024].rearrange("b p t n -> p (b t) n"),
                                 xs_quarter(i % 2, q)).then_inc(y_stored[q], 16)
                    if load_next and q > 0:
                        load(i, q - 1)
                if load_next:
                    load(i, 3)

            def load(i, q):
                sp.wait_ge(y_stored[q], (i + 1) * 16)
                sp.dma_start(xs_quarter(i % 2, q),
                             x_v[bass.ds(i + 2, 1), :, :, q * 1024:(q + 1) * 1024].rearrange("b p t n -> p (b t) n"))\
                  .then_inc(x_loaded[q], 16)

            if B > 2:
                with sp.Fori(0, B - 2) as i:
                    quarters(i, True)
            quarters(B - 2, False)
            quarters(B - 1, False)
            sp.wait_ge(s_conv, B * CH * CT)
            sp.dma_start(w1_sb, w1t.rearrange("(t p) e -> p t e", p=P)).then_inc(s_w12, 16)
            sp.dma_start(w2_sb[0:HID, :], w2t[:, :]).then_inc(s_w12, 16)
            sp.dma_start(b1_sb[0:HID, :], b1.rearrange("(e a) -> e a", a=1)).then_inc(s_w12, 16)
            sp.dma_start(b2_sb, b2.rearrange("(t p) -> p t", p=P), allow_slow_non_contiguous=True).then_inc(s_w12, 16)
            sp.wait_ge(s_scattered, 16 * NC)
            sp.dma_start(rec_sb, rec_dram.rearrange("(t p) e -> p t e", p=P)).then_inc(s_rec, 16)
            for q in range(4):
                sp.wait_ge(y_stored[q], 16 * B)

        @block.gpsimd
        def _(pool):
            pool.memset(stage_d, 0.0).then_inc(s_stage, 1)
            pool.memset(stage_rec, 0.0).then_inc(s_stage, 1)
            pool.wait_ge(s_stage, 2)
            pool.memset(stage_rec.bitcast(i32).rearrange("p (t e) -> p t e", e=REC)[:, :, 0:1], NPL)\
                .then_inc(s_stage, 1)

            def image(i):
                for c in range(CH):
                    n = i * CH + c
                    th = tpair[0:REP, c % 2, :]
                    pool.wait_ge(s_fn, n + 1)
                    if not (isinstance(i, int) and i == 0 and c < 2):
                        pool.wait_ge(s_conv, (i * CH + c - 1) * CT)
                    pool.sem_inc(s_issue, 1)
                    pool.tensor_copy(th, fn[0:REP, :]).then_inc(s_th, 1)
                    pool.wait_ge(s_th, n + 1)
                    tl = tpair[64:96, c % 2, :]
                    pool.tensor_tensor(tl, fn[64:96, :], tl, ALU.subtract).then_inc(s_t, 1)

            image(0)
            with pool.Fori(1, B) as i:
                image(i)

            pool.wait_ge(s_conv, B * CH * CT)
            pool.iota(recs[:, :, 0:1].bitcast(i32), [[C, B], [P, CT]], base=0, channel_multiplier=1).then_inc(s_iota, 1)
            pool.iota(tnum_i, [[1, NT]], base=0, channel_multiplier=0).then_inc(s_iota, 1)
            pool.wait_ge(s_iota, 2)
            pool.wait_ge(s_sorted, 1)
            pool.wait_ge(s_pad, 16)
            for j in range(NC):
                pool.indirect_dma_start(out=rec_dram[:, :], out_offset=bass.IndirectOffsetOnAxis(ap=slot_i[:, j:j + 1], axis=0),
                                        in_=recs[:, j, :], in_offset=None).then_inc(s_scattered, 16)
            pool.wait_ge(s_scattered, 16 * NC)
            for q in range(4):
                pool.wait_ge(y_stored[q], 16 * B)
            pool.memset(ypad_f, LOWEST)
            pool.memset(hbuf_f, LOWEST)
            pool.memset(small_f, LOWEST).then_inc(s_pads, 1)
            pool.wait_ge(s_rec, 16)

            def gather(t, b, first=False):
                pool.sem_inc(s_issue, 1)
                pool.tensor_copy(idx[:, b:b + 1], rec_sb[:, bass.ds(t, 1), 0].bitcast(i32)).then_inc(s_idx, 1)
                pool.wait_ge(s_idx, t + 1)
                pool.sem_inc(s_issue, 1)
                pool.indirect_dma_start(out=bufs[:, b, :], out_offset=None, in_=y_dram[:, :],
                                        in_offset=bass.IndirectOffsetOnAxis(ap=idx[:, b:b + 1], axis=0),
                                        bounds_check=NPL - 1, oob_is_err=False).then_inc(gathered[b], 16)

            def scatter(t, b):
                pool.wait_ge(s_res, (t + 1) * 8)
                pool.sem_inc(s_issue, 1)
                pool.indirect_dma_start(out=out_rows[:, :], out_offset=bass.IndirectOffsetOnAxis(ap=idx[:, b:b + 1], axis=0),
                                        in_=bufs[:, b, :], in_offset=None,
                                        bounds_check=NPL - 1, oob_is_err=False).then_inc(written[b], 16)

            def step(t, u):
                if not (isinstance(t, int) and t < 2):
                    pool.wait_ge(written[(u + 2) % BUFS], ((t - 2) // BUFS + 1) * 16 if isinstance(t, int)
                                 else turn_of(t, u - 2))
                if not (isinstance(t, int) and t + 2 >= NT):
                    gather(t + 2, (u + 2) % BUFS)
                if not (isinstance(t, int) and t < 1):
                    scatter(t - 1, (u - 1) % BUFS)

            gather(0, 0)
            gather(1, 1)
            for u in range(BUFS):
                step(u, u)
            with pool.Fori(1, NT // BUFS - 1) as g:
                def turn_of(t, back):
                    return (g + (1 if back >= 0 else 0)) * 16
                for u in range(BUFS):
                    step(g * BUFS + u, u)
            for u in range(BUFS):
                step(NT - BUFS + u, u)
            scatter(NT - 1, BUFS - 1)
            for b in range(BUFS):
                pool.wait_ge(written[b], NT // BUFS * 16)

        @block.scalar
        def _(act):
            def group_root(k):
                act.wait_ge(s_gavg, 2 * k + 2)
                act.activation(grs[:, :], psum[:, BANK_A, CT:2 * CT], ACT.Sqrt, bias=epsg[:, :]).then_inc(s_gsq, 1)

            def high_parts(i, c):
                n0 = (i * CH + c) * CT
                for ct in range(CT):
                    act.wait_ge(s_g32, n0 + ct + 1)
                    act.activation(gh[:, ct, (c % RING) * CW:(c % RING + 1) * CW], g32[:, ct % 2, :],
                                   ACT.Copy).then_inc(s_gh, 1)

            def conv_out(i, c, o):
                n = (i * CH + c) * CT + o
                act.wait_ge(s_conv, n + 1)
                if isinstance(n, int) and n < 2:
                    pass
                else:
                    act.wait_ge(s_added, n - 1)
                act.activation(relu[:, o % 2, :], psum[:, o, :], ACT.Relu, bias=bias_sb[:, o:o + 1],
                               scale=1.0 / (SC * SC)).then_inc(s_relu, 1)

            def image(i, first, last):
                for c in range(CH):
                    n = i * CH + c
                    act.wait_ge(s_pick, n + 1)
                    act.activation(frot[0:6 * KS, :], psum[0:6 * KS, BANK_A, :], ACT.Copy).then_inc(s_frot, 1)
                    if c > 0:
                        conv_out(i, c - 1, 0)
                        conv_out(i, c - 1, 1)
                    act.wait_ge(s_turn, n + 1)
                    act.activation(sq[0:D, :], psum[0:D, BANK_F, :], ACT.Square).then_inc(s_sq, 1)
                    if c > 0:
                        conv_out(i, c - 1, 2)
                        conv_out(i, c - 1, 3)
                    act.wait_ge(s_norm, n + 1)
                    act.activation(sq[0:REP, :], psum[0:REP, BANK_A, :], ACT.Sqrt,
                                   bias=epsd[0:REP, :]).then_inc(s_root, 1)
                    if c + 3 < CH:
                        high_parts(i, c + 3)
                    elif not last:
                        if c + 3 == CH:
                            group_root(i + 1)
                        high_parts(i + 1, c + 3 - CH)
                for o in range(CT):
                    conv_out(i, CH - 1, o)

            act.wait_ge(s_wsplit, 5)
            group_root(0)
            for c in range(3):
                high_parts(0, c)
            image(0, True, False)
            if B > 2:
                with act.Fori(1, B - 1) as i:
                    image(i, False, False)
            image(B - 1, False, True)

            act.wait_ge(s_smm, 2)
            act.activation(sr, psum[:, 1, 0:NC], ACT.Sqrt, bias=epsg[:, :]).then_inc(s_sroot, 1)

            def pad_plane(t, u):
                act.wait_ge(gathered[u], turns_done(t, u))
                if not (isinstance(t, int) and t == 0):
                    act.wait_ge(s_rows, t)
                act.activation(ypad[:, :, PADC:PADC + W], bufs[:, u, :].rearrange("p (h w) -> p h w", w=W),
                               ACT.Copy).then_inc(s_ypad, 1)

            def diagonals(t, s):
                if not (isinstance(t, int) and t < 2):
                    act.wait_ge(s_res, (t - 1) * 8)
                    act.wait_ge(s_rec, 16)
                for k in range(3):
                    act.activation(diag[:, s, k, :], ident, ACT.Copy, scale=rec_sb[:, bass.ds(t, 1), 1 + k])
                act.activation(const_t[:, s:s + 1], rec_sb[:, bass.ds(t, 1), 4], ACT.Copy).then_inc(s_diag, 1)

            def results(t, u):
                act.wait_ge(s_diag, t + 1)
                for b in range(8):
                    act.wait_ge(s_mix, t * 8 + b + 1)
                    act.activation(bufs[:, u, b * CW:(b + 1) * CW], psum[:, b, :], ACT.Identity,
                                   bias=const_t[:, u % 2:u % 2 + 1]).then_inc(s_res, 1)

            def turns_done(t, u):
                return (t // BUFS + 1) * 16 if isinstance(t, int) else turns[0](t, u)

            turns = [None]

            def step(t, u):
                if not (isinstance(t, int) and t + 1 >= NT):
                    pad_plane(t + 1, (u + 1) % BUFS)
                if not (isinstance(t, int) and t == 0):
                    results(t - 1, (u - 1) % BUFS)
                if not (isinstance(t, int) and t + 1 >= NT):
                    diagonals(t + 1, (u + 1) % 2)

            act.wait_ge(s_pads, 1)
            act.wait_ge(s_rec, 16)
            pad_plane(0, 0)
            diagonals(0, 0)
            for u in range(BUFS):
                step(u, u)
            with act.Fori(1, NT // BUFS - 1) as g:
                turns[0] = lambda t, u: (g + (2 if u == 0 else 1)) * 16
                for u in range(BUFS):
                    step(g * BUFS + u, u)
            for u in range(BUFS):
                step(NT - BUFS + u, u)
            results(NT - 1, BUFS - 1)

        @block.vector
        def _(dve):
            chain = [0]

            def split_weights():
                dve.memset(epsd[:, :], EPS_D * SC * SC)
                dve.memset(epsg[:, :], EPS)
                dve.wait_ge(s_const, 48)
                dve.tensor_scalar(stage_w, stage_w, SC, None, ALU.mult).then_inc(s_wsplit, 1)
                dve.wait_ge(s_wd_in, 48)
                dve.tensor_scalar(stage_d, stage_d, SC, None, ALU.mult).then_inc(s_wsplit, 1)
                dve.wait_ge(s_wsplit, 2)
                dve.tensor_copy(wh, stage_w)
                dve.tensor_copy(wd, stage_d).then_inc(s_wsplit, 1)
                dve.wait_ge(s_wsplit, 3)
                dve.tensor_tensor(wl, stage_w, wh, ALU.subtract).then_inc(s_wsplit, 1)
                dve.tensor_tensor(wd[32:64, :], stage_d[32:64, :], wd[32:64, :], ALU.subtract).then_inc(s_wsplit, 1)

            def x_stats(i, q):
                dve.wait_ge(x_loaded[q], (i + 1) * 16)
                for ct in range(CT):
                    for c in (2 * q, 2 * q + 1):
                        last = dve.bn_stats(bnx[:, ct, c, :], xs(ct, c * CW, CW, i % 2))
                if q == 3:
                    last.then_inc(s_vchain, 1)

            def group_stats(i):
                b = i * STATS_CHAIN
                dve.wait_ge(s_vchain, b + 1)
                dve.sem_inc(s_carry, 1)
                for ct in range(CT):
                    last = dve.bn_aggr(aggx[:, ct, :], bnx[:, ct, :, :].rearrange("p c s -> p (c s)"))
                last.then_inc(s_xagg, 1)
                dve.wait_ge(s_xagg, 2 * i + 1)
                dve.wait_ge(s_gavg, 2 * i + 1)
                dve.tensor_copy(gm[:, :], psum[:, BANK_A, 0:CT]).then_inc(s_vchain, 1)
                dve.wait_ge(s_vchain, b + 2)
                dve.tensor_tensor(gd[:, :], aggx[:, :, 0], gm[:, :], ALU.subtract).then_inc(s_vchain, 1)
                dve.wait_ge(s_vchain, b + 3)
                dve.tensor_tensor(gd[:, :], gd[:, :], gd[:, :], ALU.mult).then_inc(s_vchain, 1)
                dve.wait_ge(s_vchain, b + 4)
                dve.tensor_tensor(gd[:, :], gd[:, :], aggx[:, :, 1], ALU.add).then_inc(s_xagg, 1)
                dve.wait_ge(s_gsq, i + 1)
                dve.reciprocal(gd[:, :], grs[:, :]).then_inc(s_vchain, 1)
                dve.wait_ge(s_vchain, b + 5)
                if not (isinstance(i, int) and i == 0):
                    dve.wait_ge(s_g32, i * (CH * CT))
                dve.tensor_copy(gmean[:, :], gm[:, :]).then_inc(s_vchain, 1)
                dve.tensor_tensor(grs[:, :], gd[:, :], gd[:, :], ALU.mult).then_inc(s_vchain, 1)
                dve.wait_ge(s_vchain, b + 7)
                dve.scalar_tensor_tensor(grs[:, :], psum[:, BANK_A, CT:2 * CT], EPS, grs[:, :],
                                         ALU.add, ALU.mult).then_inc(s_vchain, 1)
                dve.wait_ge(s_vchain, b + 8)
                dve.tensor_scalar(grs[:, :], grs[:, :], -0.5 * SC, 1.5 * SC, ALU.mult, ALU.add).then_inc(s_newton, 1)
                dve.wait_ge(s_newton, 2 * i + 1)
                dve.tensor_tensor(grstd[:, :], grs[:, :], gd[:, :], ALU.mult).then_inc(s_newton, 1)
                dve.wait_ge(s_newton, 2 * i + 2)

            def normalise(i, c, waits=True):
                n0 = (i * CH + c) * CT
                slot = slice((c % RING) * CW, (c % RING + 1) * CW)
                if waits:
                    dve.wait_ge(s_chunk_used, i * CH + c - RING + 1)

                def low(ct):
                    dve.wait_ge(s_gh, n0 + ct + 1)
                    dve.tensor_tensor(gl[:, ct, slot], g32[:, ct % 2, :], gh[:, ct, slot],
                                      ALU.subtract).then_inc(s_gl, 1)

                for ct in range(CT):
                    if not (isinstance(n0, int) and n0 + ct < 2):
                        dve.wait_ge(s_gl, n0 + ct - 1)
                    dve.tensor_scalar(g32[:, ct % 2, :], xs(ct, c * CW, CW, i % 2), gmean[:, ct:ct + 1],
                                      grstd[:, ct:ct + 1], ALU.subtract, ALU.mult).then_inc(s_g32, 1)
                    if ct > 0:
                        low(ct - 1)
                low(CT - 1)

            def mask(i, t):
                dve.wait_ge(s_gram, i * NB + t + 1)
                runs = mask_runs(t)
                for k, run in enumerate(runs):
                    r0, n = run[0], len(run)
                    col = ((t - 1 + r0) % 8) * P
                    if n == 1:
                        dst = bq[:, r0, col:col + P]
                        src = psum[:, GRAM0 + t % 2, r0 * P:(r0 + 1) * P]
                        m = band
                    else:
                        base = bq_off + r0 * 8 * P + col
                        dst = arena[:, base:base + n * 9 * P].rearrange("p (r n) -> p r n", r=n)[:, :, 0:P]
                        src = psum[:, GRAM0 + t % 2, r0 * P:(r0 + n) * P].rearrange("p (r n) -> p r n", r=n)
                        m = band.unsqueeze(1).to_broadcast([P, n, P])
                    ins = dve.tensor_tensor(dst, src, m, ALU.mult)
                ins.then_inc(s_masked, 1)

            def residual(i, c, o):
                n = (i * CH + c) * CT + o
                y = xs(o, c * CW, CW, i % 2)
                dve.wait_ge(s_relu, n + 1)
                dve.tensor_tensor(y, y, relu[:, o % 2, :], ALU.add).then_inc(s_added, 1)
                dve.wait_ge(s_added, n + 1)
                dve.bn_stats(bny[:, o, c, :], y).then_inc(s_y, 1)

            def descriptor(i, c):
                n = i * CH + c
                dve.wait_ge(s_root, n + 1)
                if c == 0:
                    pass
                dve.reciprocal(sq[0:REP, :], sq[0:REP, :]).then_inc(s_rinv, 1)
                dve.wait_ge(s_rinv, n + 1)
                if not (isinstance(n, int) and n == 0):
                    dve.wait_ge(s_t, n)
                dve.tensor_tensor(fn[0:REP, :], psum[0:REP, BANK_F, :], sq[0:REP, :], ALU.mult).then_inc(s_fn, 1)

            def masks_of(i, c, between):
                if c == 0:
                    if not (isinstance(i, int) and i == 0):
                        dve.wait_ge(s_pick, i * CH)
                else:
                    dve.wait_ge(s_pick, i * CH + c)
                for k, t in enumerate(gram_blocks(c)):
                    mask(i, t)
                    if k < len(between):
                        between[k]()
                for f in between[len(gram_blocks(c)):]:
                    f()

            def image(i, last):
                masks_of(i, 0, [])
                for c in range(CH):
                    res = [lambda o=o: residual(i, c - 1, o) for o in range(CT)] if c > 0 else []
                    if c + 1 < CH:
                        masks_of(i, c + 1, res)
                    else:
                        for f in res:
                            f()
                    descriptor(i, c)
                    if c + 3 < CH:
                        normalise(i, c + 3, waits=not (isinstance(i, int) and i == 0 and c == 0))
                    elif not last:
                        if c + 3 == CH:
                            group_stats(i + 1)
                        normalise(i + 1, c + 3 - CH)
                    if 1 <= c <= 4 and not last:
                        x_stats(i + 1, c - 1)
                for o in range(CT):
                    residual(i, CH - 1, o)
                dve.wait_ge(s_y, (i + 1) * CH * CT)
                dve.sem_inc(s_carry, 1)
                for ct in range(CT):
                    ins = dve.bn_aggr(aggy[:, ct, :], bny[:, ct, :, :].rearrange("p c s -> p (c s)"))
                ins.then_inc(s_yagg, 1)
                dve.wait_ge(s_yagg, i + 1)
                dve.tensor_copy(ymv[:, bass.ds(i * (2 * CT), 2 * CT)],
                                aggy[:, :, :].rearrange("p t s -> p (t s)")).then_inc(s_ymv, 1)

            def sort_planes():
                links = [0]

                def link(ins):
                    links[0] += 1
                    ins.then_inc(s_link, 1)
                    dve.wait_ge(s_link, links[0])

                stats = ymv[:, :].rearrange("p (n s) -> p n s", s=2)
                dve.wait_ge(s_ymv, B)
                dve.wait_ge(s_conv, B * CH * CT)
                dve.memset(zeros, 0.0)
                dve.tensor_copy(sm, stats[:, :, 0]).then_inc(s_sstat, 1)
                dve.wait_ge(s_smm, 1)
                link(dve.tensor_tensor(sd, sm, psum[:, 0, 0:NC], ALU.subtract))
                link(dve.tensor_tensor(tmp, sd, sd, ALU.mult))
                dve.tensor_tensor(tmp, tmp, stats[:, :, 1], ALU.add).then_inc(s_sstat, 1)
                dve.wait_ge(s_sroot, 1)
                link(dve.reciprocal(sa, sr))
                link(dve.tensor_tensor(sr, sa, sa, ALU.mult))
                link(dve.scalar_tensor_tensor(sr, psum[:, 1, 0:NC], EPS, sr, ALU.add, ALU.mult))
                link(dve.tensor_scalar(sr, sr, -0.5, 1.5, ALU.mult, ALU.add))
                link(dve.tensor_tensor(sa, sr, sa, ALU.mult))
                link(dve.scalar_tensor_tensor(scc, psum[:, 0, 0:NC], -1.0, sa, ALU.mult, ALU.mult))
                dve.tensor_tensor(sgap, sd, sa, ALU.mult).then_inc(s_sstat, 1)
                dve.wait_ge(s_w12, 64)
                dve.wait_ge(s_smm, 3)
                dve.tensor_scalar(hid[0:HID, :], psum[0:HID, 2, 0:B], b1_sb[0:HID, :], 0.0, ALU.add, ALU.max)\
                    .then_inc(s_sstat, 1)
                dve.wait_ge(s_smm, 4)
                link(dve.tensor_tensor(score.rearrange("p (b t) -> p b t", t=CT),
                                       psum[:, 3, 0:NC].rearrange("p (t b) -> p b t", t=CT),
                                       b2_sb.unsqueeze(1).to_broadcast([P, B, CT]), ALU.add))
                link(dve.tensor_scalar(score, score, 0.0, None, ALU.max))
                link(dve.tensor_scalar(cls, score, 1.0, None, ALU.is_ge))
                for k in range(2, NCLS):
                    link(dve.scalar_tensor_tensor(cls, score, float(k), cls, ALU.is_ge, ALU.add))
                for k in range(NCLS):
                    ins = dve.tensor_scalar(onehot[:, k * NC:(k + 1) * NC], cls, float(k), None, ALU.is_equal)
                ins.then_inc(s_sstat, 1)
                link(dve.scalar_tensor_tensor(fs, cls, 1.0, score, ALU.add, ALU.subtract))
                link(dve.tensor_tensor(fb, score, cls, ALU.subtract))
                dve.wait_ge(s_iota, 2)
                dve.tensor_scalar(recs[:, :, 1], sa, 1.0, None, ALU.add)
                dve.tensor_tensor(recs[:, :, 2], fs, sa, ALU.mult)
                dve.tensor_tensor(recs[:, :, 3], fb, sa, ALU.mult)
                link(dve.scalar_tensor_tensor(tmp, fs, 1.0, fb, ALU.add, ALU.add))
                dve.tensor_tensor(recs[:, :, 4], tmp, scc, ALU.mult)
                dve.memset(recs[:, :, 5:REC], 0.0)
                dve.wait_ge(s_smm, 6)
                for k in range(NCLS):
                    cols = slice(k * NC, (k + 1) * NC)
                    ins = dve.tensor_tensor_scan(incl[:, cols], psum[:, 5, cols], zeros, 0.0, ALU.add, ALU.add)
                link(ins)
                link(dve.tensor_tensor(rank, incl, psum[:, 5, 0:NCLS * NC], ALU.subtract))
                link(dve.tensor_tensor(rank, rank, psum[:, 4, 0:NCLS * NC], ALU.add))
                totals = incl.rearrange("p (k n) -> p k n", k=NCLS)[:, :, NC - 1]
                link(dve.tensor_scalar(tiles, totals, 1.0 / P, 0.5 - 0.5 / P, ALU.mult, ALU.add))
                link(dve.tensor_scalar(tiles, tiles, 2.0 ** 23, None, ALU.add))
                link(dve.tensor_scalar(tiles, tiles, -2.0 ** 23, None, ALU.add))
                link(dve.tensor_tensor_scan(tincl, tiles, zeros[:, 0:NCLS], 0.0, ALU.add, ALU.add))
                link(dve.tensor_tensor(tbase, tincl, tiles, ALU.subtract))
                link(dve.tensor_scalar(tb128, tbase, float(P), None, ALU.mult))
                for k in range(NCLS):
                    cols = slice(k * NC, (k + 1) * NC)
                    ins = dve.scalar_tensor_tensor(rank[:, cols], rank[:, cols], tb128[:, k:k + 1], onehot[:, cols],
                                                   ALU.add, ALU.mult)
                link(ins)
                link(dve.tensor_reduce(slot_f, rank.rearrange("p (k n) -> p n k", k=NCLS), AX.X, ALU.add))
                dve.tensor_copy(slot_i, slot_f)
                link(dve.tensor_copy(tnum, tnum_i))
                link(dve.tensor_scalar(tcls, tnum, tincl[:, 0:1], None, ALU.is_ge))
                for k in range(1, NCLS):
                    link(dve.scalar_tensor_tensor(tcls, tnum, tincl[:, k:k + 1], tcls, ALU.is_ge, ALU.add))
                dve.tensor_copy(cls_i, tcls).then_inc(s_sorted, 1)

            OWN = 20

            def pools(t, s, k):
                used = [0]

                def op(dst, a, b, wait=True, signal=s_own):
                    if wait and used[0]:
                        dve.wait_ge(s_own, t * OWN + used[0])
                    ins = dve.tensor_tensor(dst, a, b, ALU.max)
                    ins.then_inc(signal, 1)
                    if signal is s_own:
                        used[0] += 1

                def window(src, mid, dst, r, signal=s_own):
                    m, w = half_m, half_w
                    n = 31 + r
                    op(mid(m, 0, n), src(1 - r, n), src(2 - r, n))
                    core = m
                    if r >= 2:
                        op(mid(w, 0, n - 1), mid(m, 0, n - 1), mid(m, 1, n - 1))
                        core = w
                    if r == 3:
                        op(mid(m, 0, 32), mid(w, 0, 32), mid(w, 1, 32))
                        core = m
                    if r >= 4:
                        op(mid(m, 0, 32), mid(w, 0, 32), mid(w, 2, 32))
                        core = m
                    if r == 5:
                        op(mid(m, 0, 32), mid(m, 0, 32), mid(w, 3, 32))
                    op(dst(0), mid(core, 0, 32), src(-r, 32))
                    op(dst(1), mid(core, 0, 32), src(1 + r, 32), wait=False, signal=signal)

                def cols(i, n):
                    return ypad[:, :, PADC + i:PADC + i + 2 * n - 1:2]

                def cols_mid(a, i, n):
                    return a.rearrange("p (h w) -> p h w", w=36)[:, :, i:i + n]

                def rows(i, n):
                    return hbuf[:, PADC + i:PADC + i + 2 * n - 1:2, :]

                def rows_mid(a, i, n):
                    return a.rearrange("p (h w) -> p h w", w=W)[:, i:i + n, :]

                sm_, bg = small[:, s, :, :], big[:, s, :].rearrange("p (h w) -> p h w", w=W)
                inner = hbuf[:, PADC:PADC + H, :]
                if k == 0:
                    window(cols, cols_mid, lambda e: inner[:, :, e::2], 1)
                    dve.tensor_copy(sm_[:, :, 1:W + 1], ypad[:, :, PADC:PADC + W]).then_inc(s_rows, 1)
                    window(rows, rows_mid, lambda e: bg[:, e::2, :], 1, signal=s_pool)
                else:
                    window(cols, cols_mid, lambda e: inner[:, :, e::2], k, signal=s_rows)
                    dve.wait_ge(s_rows, t + 1)
                    window(rows, rows_mid, lambda e: sm_[:, e::2, 1:W + 1], k)
                    op(inner, sm_[:, :, 0:W], sm_[:, :, 2:W + 2])
                    op(bg, hbuf[:, PADC - 1:PADC - 1 + H, :], hbuf[:, PADC + 1:PADC + 1 + H, :], signal=s_pool)
                assert used[0] <= OWN
                dve.sem_inc(s_own, OWN - used[0])

            def tile(t, s):
                cls_t = dve.value_load(cls_i[0:1, bass.ds(t, 1)], min_val=0, max_val=NCLS)

                def waits():
                    dve.wait_ge(s_ypad, t + 1)
                    if not (isinstance(t, int) and t < 2):
                        dve.wait_ge(s_mix, (t - 1) * 8)
                    if not (isinstance(t, int) and t == 0):
                        dve.wait_ge(s_pool, t)

                def branch(lo, hi):
                    if lo == hi:
                        waits()
                        if lo == NCLS:
                            dve.sem_inc(s_own, OWN)
                            dve.sem_inc(s_rows, 1)
                            dve.sem_inc(s_pool, 1)
                        else:
                            pools(t, s, lo)
                        return
                    mid = (lo + hi) // 2
                    with dve.If(cls_t < mid + 1):
                        branch(lo, mid)
                    with dve.Else():
                        branch(mid + 1, hi)

                branch(0, NCLS)

            split_weights()
            for q in range(4):
                x_stats(0, q)
            group_stats(0)
            for c in range(3):
                normalise(0, c, waits=False)
            image(0, False)
            if B > 2:
                with dve.Fori(1, B - 1) as i:
                    image(i, False)
            image(B - 1, True)
            sort_planes()
            dve.wait_ge(s_pads, 1)
            for t in range(2):
                tile(t, t)
            with dve.Fori(1, NT // 2) as g:
                for s in range(2):
                    tile(g * 2 + s, s)

        @block.tensor
        def _(pe):
            def product(dst, w, m, k, nk):
                return pe.matmul(dst, w, m, start=(k == 0), stop=(k == nk - 1))

            def gram(i, t):
                if not (isinstance(i, int) and i == 0 and t < 2):
                    pe.wait_ge(s_masked, i * NB + t - 1)
                own = ((2 * t) % (RING * ROWS)) * W
                for col, ring, n in gram_parts(t):
                    for ct in range(CT):
                        sh, sl = gh[:, ct, own:own + 2 * W], gl[:, ct, own:own + 2 * W]
                        mh, ml = gh[:, ct, ring:ring + n], gl[:, ct, ring:ring + n]
                        dst = psum[:, GRAM0 + t % 2, col:col + n]
                        product(dst, sh, mh, 3 * ct, 3 * CT)
                        product(dst, sh, ml, 3 * ct + 1, 3 * CT)
                        last = product(dst, sl, mh, 3 * ct + 2, 3 * CT)
                last.then_inc(s_gram, 1)

            def conv(i, c, o):
                if not (isinstance(i, int) and i == 0 and c == 0):
                    pe.wait_ge(s_relu, (i * CH + c - 1) * CT + o + 1)
                slot = slice((c % RING) * CW, (c % RING + 1) * CW)
                for ct in range(CT):
                    h, l = wh[:, ct, o * P:(o + 1) * P], wl[:, ct, o * P:(o + 1) * P]
                    dst = psum[:, o, :]
                    pe.matmul(dst, h, gh[:, ct, slot], start=(ct == 0), stop=False)
                    pe.matmul(dst, h, gl[:, ct, slot], start=False, stop=False)
                    last = pe.matmul(dst, l, gh[:, ct, slot], start=False, stop=False)
                if o == CT - 1:
                    last.then_inc(s_chunk_used, 1)

            def picks(i, c, last):
                pe.wait_ge(s_masked, i * NB + gram_blocks(c)[-1] + 1)
                if not (isinstance(i, int) and i == 0 and c == 0):
                    pe.wait_ge(s_root, i * CH + c)
                if isinstance(i, int) and i == 0 and c == 0:
                    pe.wait_ge(s_vchain, STATS_CHAIN)
                if c == 6 and not last:
                    pe.wait_ge(s_vchain, (i + 2) * STATS_CHAIN)
                half = (c % 2) * 4 * P
                dst = psum[0:6 * KS, BANK_A, :]
                pe.matmul(dst, pick[:, 1, :], bq[:, 1, half:half + 4 * P], start=True, stop=False)
                lo = P if c == 0 else 0
                pe.matmul(dst[:, lo:], pick[:, 2, :], bq[:, 2, half + lo:half + 4 * P], start=False, stop=False)
                hi = 3 * P if c == CH - 1 else 4 * P
                pe.matmul(dst[:, 0:hi], pick[:, 0, :], bq[:, 0, half:half + hi], start=False, stop=True)\
                  .then_inc(s_pick, 1)

            def turns(i, c):
                pe.wait_ge(s_frot, i * CH + c + 1)
                if not (isinstance(i, int) and i == 0 and c == 0):
                    pe.wait_ge(s_fn, i * CH + c)
                src = frot[0:6 * KS, :].rearrange("p (r e w) -> p r e w", e=2, w=W)
                dst = psum[0:REP, BANK_F, :].rearrange("p (r e w) -> p r e w", e=2, w=W)
                for e in range(2):
                    for k in range(KS):
                        last = pe.matmul(dst[:, :, e, k::KS], turn[0:6 * KS, e, k, :], src[:, :, e, k::KS],
                                         start=True, stop=True)
                last.then_inc(s_turn, 1)

            def norm(i, c):
                pe.wait_ge(s_sq, i * CH + c + 1)
                pe.matmul(psum[0:REP, BANK_A, :], ssum[0:D, :], sq[0:D, :], start=True, stop=True)\
                  .then_inc(s_norm, 1)

            def tail(i, c):
                pe.wait_ge(s_t, i * CH + c + 1)
                for o in range(CT):
                    pe.matmul(psum[:, o, :], wd[0:REP, o * P:(o + 1) * P], tpair[0:REP, c % 2, :],
                              start=False, stop=True).then_inc(s_conv, 1)

            def group_average(i):
                pe.wait_ge(s_xagg, 2 * i + 1)
                if not (isinstance(i, int) and i == 0):
                    pe.wait_ge(s_root, i * CH - 2)
                pe.matmul(psum[:, BANK_A, 0:CT], gavg, aggx[:, :, 0], start=True, stop=True).then_inc(s_gavg, 1)

            def group_spread(i):
                pe.wait_ge(s_xagg, 2 * i + 2)
                pe.matmul(psum[:, BANK_A, CT:2 * CT], gavg, gd[:, :], start=True, stop=True).then_inc(s_gavg, 1)

            def image(i, last):
                pe.wait_ge(s_gl, (i * CH + 2) * CT)
                for t in gram_blocks(0):
                    gram(i, t)
                for c in range(CH):
                    if c + 1 < CH:
                        fill = [lambda t=t: gram(i, t) for t in gram_blocks(c + 1)]
                        convs = list(range(CT))
                    else:
                        fill = []
                        convs = list(range(CT))
                    if c == 0:
                        conv(i, c, convs.pop(0))
                    picks(i, c, last)
                    if c + 1 < CH:
                        pe.wait_ge(s_gl, (i * CH + min(c + 3, CH)) * CT)
                        fill[0](); fill[1]()
                    else:
                        conv(i, c, convs.pop(0))
                    turns(i, c)
                    if c + 1 < CH:
                        for f in fill[2:]:
                            f()
                    else:
                        conv(i, c, convs.pop(0))
                    norm(i, c)
                    for n, o in enumerate(convs):
                        conv(i, c, o)
                        if c == 5 and not last and n == 0:
                            group_average(i + 1)
                        if c == 5 and not last and n == 1:
                            group_spread(i + 1)
                    tail(i, c)

            pe.wait_ge(s_wsplit, 5)
            group_average(0)
            group_spread(0)
            image(0, False)
            if B > 2:
                with pe.Fori(1, B - 1) as i:
                    image(i, False)
            image(B - 1, True)

            stats = ymv[:, :].rearrange("p (n s) -> p n s", s=2)
            pe.wait_ge(s_relu, B * CH * CT)
            pe.wait_ge(s_sstat, 1)
            pe.matmul(psum[:, 0, 0:NC], gavg, sm, start=True, stop=True).then_inc(s_smm, 1)
            pe.wait_ge(s_sstat, 2)
            pe.matmul(psum[:, 1, 0:NC], gavg, tmp, start=True, stop=True).then_inc(s_smm, 1)
            pe.wait_ge(s_sstat, 3)
            pe.wait_ge(s_w12, 64)
            gap = sgap.rearrange("p (b t) -> p b t", t=CT)
            for ct in range(CT):
                last = product(psum[0:HID, 2, 0:B], w1_sb[:, ct, :], gap[:, :, ct], ct, CT)
            last.then_inc(s_smm, 1)
            pe.wait_ge(s_sstat, 4)
            for ct in range(CT):
                last = pe.matmul(psum[:, 3, ct * B:(ct + 1) * B], w2_sb[0:HID, ct * P:(ct + 1) * P], hid[0:HID, :],
                                 start=True, stop=True)
            last.then_inc(s_smm, 1)
            pe.wait_ge(s_sstat, 5)
            pe.matmul(psum[:, 4, 0:NCLS * NC], before, onehot, start=True, stop=True).then_inc(s_smm, 1)
            pe.matmul(psum[:, 5, 0:NCLS * NC], ones, onehot, start=True, stop=True).then_inc(s_smm, 1)

            def mix(t, u):
                s = u % 2
                pe.wait_ge(s_diag, t + 1)
                pe.wait_ge(s_pool, t + 1)
                for b in range(8):
                    if not (isinstance(t, int) and t == 0):
                        pe.wait_ge(s_res, (t - 1) * 8 + b + 1)
                    dst = psum[:, b, :]
                    pe.matmul(dst, diag[:, s, 0, :], bufs[:, u, b * CW:(b + 1) * CW], start=True, stop=False)
                    pe.matmul(dst, diag[:, s, 1, :], small[:, s, b * ROWS:(b + 1) * ROWS, 1:W + 1],
                              start=False, stop=False)
                    pe.matmul(dst, diag[:, s, 2, :], big[:, s, b * CW:(b + 1) * CW], start=False, stop=True)\
                      .then_inc(s_mix, 1)

            pe.wait_ge(s_sorted, 1)
            for u in range(BUFS):
                mix(u, u)
            with pe.Fori(1, NT // BUFS) as g:
                for u in range(BUFS):
                    mix(g * BUFS + u, u)


def kernel(x, L0_conv_W, L0_conv_bias, L1_conv_w1, L1_conv_b1, L1_conv_w2, L1_conv_b2):
    import concourse.bacc as _bacc
    from concourse.bass_utils import run_bass_kernel_spmd as _run

    nc = _bacc.Bacc("TRN2", target_bir_lowering=False, num_devices=1)
    ins = {
        "x": x, "wt": L0_conv_W.T, "bias": L0_conv_bias, "w1t": L1_conv_w1.T, "b1": L1_conv_b1,
        "w2t": L1_conv_w2.T, "b2": L1_conv_b2, "consts": const_arrays(),
    }
    arrays, args = {}, []
    for name, a in ins.items():
        a = np.ascontiguousarray(a)
        arrays[f"in_{name}"] = a
        args.append(nc.dram_tensor(f"in_{name}", a.shape, mybir.dt.from_np(a.dtype), kind="ExternalInput").ap())
    out = nc.dram_tensor("out", x.shape, mybir.dt.float32, kind="ExternalOutput").ap()
    build(nc, *args, out)
    r = _run(nc, [arrays], core_ids=[0])
    return r.results[0]["out"]
```

```python
import numpy as np
from contextlib import ExitStack

import concourse.bass as bass
from concourse import mybir

P = 128
C, H, W = 512, 64, 64
PIX = H * W
CT = C // P
ROWS = 8
CH = H // ROWS
CW = ROWS * W
NB = H // 2
PAIRS = ROWS // 2
PRING = 2 * PAIRS
AFTER, SAME, BEFORE = range(3)
KS = 5
D = KS * KS
CG = 16
HID = 32
NCLS = 6
SC = 64.0
EPS = 1e-5
EPS_D = 1e-6
RING = 4
LOWEST = -3.4028234663852886e38
PADC = 6
REC = 8
BUFS = 4
REP = 3 * 32


def const_arrays():
    p = np.arange(P)
    r, w = p // W, p % W
    q = np.arange(2 * W)
    band = (np.abs(w[:, None] - (q % W)[None, :]) <= KS // 2).astype(np.float32)
    pick = np.zeros((P, 3, 2, REP), np.float32)
    for role in range(3):
        for e in range(2):
            di = r + 2 * (1 - role) - e
            ok = np.abs(di) <= KS // 2
            for rep in range(3):
                pick[p[ok], role, e, (32 * rep + (di + 2) * KS + w % KS)[ok]] = 1.0
    ssum = np.zeros((P, REP), np.float32)
    ssum[:D] = 2.0 ** -12
    gavg = (p[:, None] // CG == p[None, :] // CG).astype(np.float32) / CG
    ident = np.eye(P, dtype=np.float32)
    before = (p[:, None] < p[None, :]).astype(np.float32)
    ones = np.ones((P, P), np.float32)
    return np.concatenate([band, pick.reshape(P, -1), ssum, gavg, ident, before, ones], axis=1)


CONST_W = 2 * W + 3 * 2 * REP + REP + 4 * P


def turned_rows():
    rows = np.zeros((D, KS), np.int64)
    for k in range(KS):
        for di in range(KS):
            for dj in range(-2, 3):
                rows[di * KS + (k + dj) % KS, k] = C + di * KS + dj + 2
    return rows


def build(nc, x, wt, wturn, bias, w1t, b1, w2t, b2, consts, out):
    fp32, fp16, i32 = mybir.dt.float32, mybir.dt.float16, mybir.dt.int32
    ALU, ACT, AX = mybir.AluOpType, mybir.ActivationFunctionType, mybir.AxisListType
    B = x.shape[0]
    NC = B * CT
    NPL = NC * P
    NT = -(-(NC + NCLS - 1) // BUFS) * BUFS
    assert B >= 2
    nc.disable_value_cache = True

    x_v = x.rearrange("b (t p) h w -> b p t (h w)", p=P)
    out_rows = out.rearrange("b c h w -> (b c) (h w)")
    y_dram = nc.dram_tensor("y_planes", [NPL, PIX], fp32, kind="Internal").ap()
    y_v = y_dram.rearrange("(b t p) n -> b p t n", t=CT, p=P)
    rec_dram = nc.dram_tensor("plane_records", [NT * P, REC], fp32, kind="Internal").ap()

    ctx = ExitStack()
    with ctx:
        def sem(name):
            return ctx.enter_context(nc.semaphore(name))

        def sb(name, shape, dt):
            return ctx.enter_context(nc.sbuf_tensor(name, shape, dt))

        cst = sb("cst", [P, CONST_W], fp32)
        o = 0
        band = cst[:, o:o + 2 * W]; o += 2 * W
        pick = cst[:, o:o + 6 * REP].rearrange("p (r e m) -> p r e m", r=3, e=2); o += 6 * REP
        ssum = cst[:, o:o + REP]; o += REP
        gavg = cst[:, o:o + P]; o += P
        ident = cst[:, o:o + P]; o += P
        before = cst[:, o:o + P]; o += P
        ones = cst[:, o:o + P]; o += P
        bias_sb = sb("bias_sb", [P, CT], fp32)
        epsd = sb("epsd", [P, 1], fp32)
        epsg = sb("epsg", [P, 1], fp32)
        bnx = sb("bnx", [P, CT, CH, 6], fp32)
        bny = sb("bny", [P, CT, CH, 6], fp32)
        aggx = sb("aggx", [P, CT, 2], fp32)
        aggy = sb("aggy", [P, CT, 2], fp32)
        ymv = sb("ymv", [P, B * CT * 2], fp32)
        gm = sb("gm", [P, CT], fp32)
        gd = sb("gd", [P, CT], fp32)
        grs = sb("grs", [P, CT], fp32)
        gbias = sb("gbias", [P, CT], fp32)
        grstd = sb("grstd", [P, CT], fp32)

        ARENA = 50944
        arena = sb("arena", [P, ARENA], fp32)
        pos = [0]

        def take(n):
            pos[0] += n
            assert pos[0] <= ARENA
            return arena[:, pos[0] - n:pos[0]]

        take(2 * CT * PIX)
        gh = take(CT * RING * CW // 2).bitcast(fp16).rearrange("p (t n) -> p t n", t=CT)
        gl = take(CT * RING * CW // 2).bitcast(fp16).rearrange("p (t n) -> p t n", t=CT)
        sort_scratch = arena[:, 2 * CT * PIX:2 * CT * PIX + CT * RING * CW]
        g32 = take(2 * CW).rearrange("p (s n) -> p s n", s=2)
        bq_off = pos[0]
        bq = take(3 * PRING * P).rearrange("p (r n) -> p r n", r=3)
        sq = take(CW)
        fn = take(CW)
        tpair = take(CW).bitcast(fp16).rearrange("p (s n) -> p s n", s=2)
        relu = take(2 * CW).rearrange("p (s n) -> p s n", s=2)
        wh = take(CT * C // 2).bitcast(fp16).rearrange("p (t n) -> p t n", t=CT)
        wl = take(CT * C // 2).bitcast(fp16).rearrange("p (t n) -> p t n", t=CT)
        wd = take(KS * C // 2).bitcast(fp16)
        stage_w = arena[:, CT * PIX:CT * PIX + CT * C].rearrange("p (t n) -> p t n", t=CT)
        stage_d = arena[:, CT * PIX + CT * C:CT * PIX + (CT + KS) * C]
        stage_rec = arena[:, CT * PIX + (CT + KS) * C:CT * PIX + (CT + KS) * C + NT * REC]


        def xs_quarter(par, q):
            return arena[:, bass.ds(par * (CT * PIX), CT * PIX)]\
                .rearrange("p (t n) -> p t n", t=CT)[:, :, q * (PIX // 4):(q + 1) * (PIX // 4)]

        pos[0] = 2 * CT * PIX
        v = lambda n: take(n)
        w1_sb = v(CT * HID).rearrange("p (t e) -> p t e", t=CT)
        w2_sb = v(C)
        b1_sb = v(1)
        b2_sb = v(CT)
        sm, sd, sa, sr, scc, sgap = (v(NC) for _ in range(6))
        score, cls, fs, fb, tmp = (v(NC) for _ in range(5))
        hid = v(B)
        onehot = v(NCLS * NC)
        incl = v(NCLS * NC)
        rank = v(NCLS * NC)
        zeros = v(NC)
        tiles, tincl, tbase, tb128 = (v(NCLS) for _ in range(4))
        slot_f = v(NC)
        slot_i = v(NC).bitcast(i32)
        tnum_i = v(NT).bitcast(i32)
        tnum = v(NT)
        tcls = v(NT)
        recs = v(NC * REC).rearrange("p (n e) -> p n e", e=REC)
        assert pos[0] <= 2 * CT * PIX + CT * RING * CW
        pos[0] = 0
        bufs = v(BUFS * PIX).rearrange("p (b n) -> p b n", b=BUFS)
        WP = W + 2 * PADC
        ypad_f = v(H * WP)
        ypad = ypad_f.rearrange("p (h w) -> p h w", w=WP)
        hbuf_f = v((H + 2 * PADC) * W)
        hbuf = hbuf_f.rearrange("p (h w) -> p h w", w=W)
        small_f = v(2 * H * (W + 2))
        small = small_f.rearrange("p (s h w) -> p s h w", s=2, h=H)
        big = v(2 * PIX).rearrange("p (s n) -> p s n", s=2)
        half_m, half_w = v(36 * W), v(36 * W)
        rec_sb = v(NT * REC).rearrange("p (t e) -> p t e", e=REC)
        diag = v(2 * 3 * P).rearrange("p (s k n) -> p s k n", s=2, k=3)
        cls_i = v(NT).bitcast(i32)
        idx = v(BUFS).bitcast(i32)
        const_t = v(2)

        psum = ctx.enter_context(nc.psum_tensor("psum", [P, 8, 512], fp32))
        GRAM0, BANK_A, BANK_N = 4, 6, 7

        s_const = sem("s_const")
        s_stage = sem("s_stage")
        s_wd_in = sem("s_wd_in")
        s_pad = sem("s_pad")
        s_wsplit = sem("s_wsplit")
        x_loaded = [sem(f"x_loaded{q}") for q in range(4)]
        y_stored = [sem(f"y_stored{q}") for q in range(4)]
        s_xagg = sem("s_xagg")
        s_gavg = sem("s_gavg")
        s_gsq = sem("s_gsq")
        s_vchain = sem("s_vchain")
        s_carry_a = sem("s_carry_a")
        s_gh = sem("s_gh")
        s_gl = sem("s_gl")
        s_chunk_used = sem("s_chunk_used")
        s_gram = sem("s_gram")
        s_masked = sem("s_masked")
        s_turned = sem("s_turned")
        s_after = sem("s_after")
        s_pick = sem("s_pick")
        s_sq = sem("s_sq")
        s_norm = sem("s_norm")
        s_root = sem("s_root")
        s_rinv = sem("s_rinv")
        s_fn = sem("s_fn")
        s_th = sem("s_th")
        s_t = sem("s_t")
        s_conv = sem("s_conv")
        s_relu = sem("s_relu")
        s_added = sem("s_added")
        s_y = sem("s_y")
        s_ymv = sem("s_ymv")
        s_yagg = sem("s_yagg")
        s_newton = sem("s_newton")
        s_issue = sem("s_issue")
        s_carry = sem("s_carry")
        s_w12 = sem("s_w12")
        s_link = sem("s_link")
        s_sstat = sem("s_sstat")
        s_smm = sem("s_smm")
        s_sroot = sem("s_sroot")
        s_iota = sem("s_iota")
        s_sorted = sem("s_sorted")
        s_scattered = sem("s_scattered")
        s_rec = sem("s_rec")
        s_pads = sem("s_pads")
        s_idx = sem("s_idx")
        gathered = [sem(f"gathered{b}") for b in range(BUFS)]
        written = [sem(f"written{b}") for b in range(BUFS)]
        s_ypad = sem("s_ypad")
        s_rows = sem("s_rows")
        s_own = sem("s_own")
        s_pool = sem("s_pool")
        s_diag = sem("s_diag")
        s_mix = sem("s_mix")
        s_res = sem("s_res")

        block = ctx.enter_context(nc.Block())

        STATS_CHAIN = 7

        def xs(ct, lo, n, par):
            return arena[:, bass.ds(par * (CT * PIX) + (ct * PIX + lo), n)]

        def gram_parts(t):
            parts, row = [], 2 * t
            while row < min(2 * t + 4, H):
                end = min(2 * t + 4, H, (row // (RING * ROWS) + 1) * RING * ROWS)
                parts.append(((row - 2 * t) * W, (row % (RING * ROWS)) * W, (end - row) * W))
                row = end
            return parts

        @block.sync
        def _(sp):
            sp.dma_start(cst[:, :], consts[:, :]).then_inc(s_const, 16)
            sp.dma_start(bias_sb[:, :], bias.rearrange("(t p) -> p t", p=P),
                         allow_slow_non_contiguous=True).then_inc(s_const, 16)
            sp.dma_start(stage_w, wt[0:C, :].rearrange("(t p) n -> p t n", p=P)).then_inc(s_const, 16)
            for q in range(4):
                sp.dma_start(xs_quarter(0, q), x_v[0, :, :, q * 1024:(q + 1) * 1024]).then_inc(x_loaded[q], 16)
            sp.wait_ge(s_stage, 3)
            for rep in range(3):
                sp.dma_start(stage_d[32 * rep:32 * rep + D, :], wturn[:, :]).then_inc(s_wd_in, 16)
            sp.dma_start(rec_dram.rearrange("(t p) e -> p t e", p=P),
                         stage_rec.rearrange("p (t e) -> p t e", e=REC)).then_inc(s_pad, 16)

            sp.wait_ge(s_wsplit, 5)
            sp.wait_ge(s_pad, 16)
            for q in range(4):
                sp.dma_start(xs_quarter(1, q), x_v[1, :, :, q * 1024:(q + 1) * 1024]).then_inc(x_loaded[q], 16)

            def quarters(i, load_next):
                for q in range(4):
                    sp.wait_ge(s_y, i * (CH * CT) + (q + 1) * 2 * CT)
                    sp.dma_start(y_v[bass.ds(i, 1), :, :, q * 1024:(q + 1) * 1024].rearrange("b p t n -> p (b t) n"),
                                 xs_quarter(i % 2, q)).then_inc(y_stored[q], 16)
                    if load_next and q > 0:
                        load(i, q - 1)
                if load_next:
                    load(i, 3)

            def load(i, q):
                sp.wait_ge(y_stored[q], (i + 1) * 16)
                sp.dma_start(xs_quarter(i % 2, q),
                             x_v[bass.ds(i + 2, 1), :, :, q * 1024:(q + 1) * 1024].rearrange("b p t n -> p (b t) n"))\
                  .then_inc(x_loaded[q], 16)

            if B > 2:
                with sp.Fori(0, B - 2) as i:
                    quarters(i, True)
            quarters(B - 2, False)
            quarters(B - 1, False)
            sp.wait_ge(s_conv, B * CH * CT)
            sp.dma_start(w1_sb, w1t.rearrange("(t p) e -> p t e", p=P)).then_inc(s_w12, 16)
            sp.dma_start(w2_sb[0:HID, :], w2t[:, :]).then_inc(s_w12, 16)
            sp.dma_start(b1_sb[0:HID, :], b1.rearrange("(e a) -> e a", a=1)).then_inc(s_w12, 16)
            sp.dma_start(b2_sb, b2.rearrange("(t p) -> p t", p=P), allow_slow_non_contiguous=True).then_inc(s_w12, 16)
            sp.wait_ge(s_scattered, 16 * NC)
            sp.dma_start(rec_sb, rec_dram.rearrange("(t p) e -> p t e", p=P)).then_inc(s_rec, 16)
            for q in range(4):
                sp.wait_ge(y_stored[q], 16 * B)

        @block.gpsimd
        def _(pool):
            pool.memset(stage_d, 0.0).then_inc(s_stage, 1)
            pool.memset(stage_rec, 0.0).then_inc(s_stage, 1)
            pool.wait_ge(s_stage, 2)
            pool.memset(stage_rec.bitcast(i32).rearrange("p (t e) -> p t e", e=REC)[:, :, 0:1], NPL)\
                .then_inc(s_stage, 1)

            def image(i):
                for c in range(CH):
                    n = i * CH + c
                    th = tpair[0:REP, c % 2, :]
                    pool.wait_ge(s_fn, n + 1)
                    if not (isinstance(i, int) and i == 0 and c < 2):
                        pool.wait_ge(s_conv, (i * CH + c - 1) * CT)
                    pool.sem_inc(s_issue, 1)
                    pool.tensor_copy(th, fn[0:REP, :]).then_inc(s_th, 1)
                    pool.wait_ge(s_th, n + 1)
                    tl = tpair[64:96, c % 2, :]
                    pool.tensor_tensor(tl, fn[64:96, :], tl, ALU.subtract).then_inc(s_t, 1)

            image(0)
            with pool.Fori(1, B) as i:
                image(i)

            pool.wait_ge(s_conv, B * CH * CT)
            pool.iota(recs[:, :, 0:1].bitcast(i32), [[C, B], [P, CT]], base=0, channel_multiplier=1).then_inc(s_iota, 1)
            pool.iota(tnum_i, [[1, NT]], base=0, channel_multiplier=0).then_inc(s_iota, 1)
            pool.wait_ge(s_iota, 2)
            pool.wait_ge(s_sorted, 1)
            pool.wait_ge(s_pad, 16)
            for j in range(NC):
                pool.indirect_dma_start(out=rec_dram[:, :], out_offset=bass.IndirectOffsetOnAxis(ap=slot_i[:, j:j + 1], axis=0),
                                        in_=recs[:, j, :], in_offset=None).then_inc(s_scattered, 16)
            pool.wait_ge(s_scattered, 16 * NC)
            for q in range(4):
                pool.wait_ge(y_stored[q], 16 * B)
            pool.memset(ypad_f, LOWEST)
            pool.memset(hbuf_f, LOWEST)
            pool.memset(small_f, LOWEST).then_inc(s_pads, 1)
            pool.wait_ge(s_rec, 16)

            def gather(t, b, first=False):
                pool.sem_inc(s_issue, 1)
                pool.tensor_copy(idx[:, b:b + 1], rec_sb[:, bass.ds(t, 1), 0].bitcast(i32)).then_inc(s_idx, 1)
                pool.wait_ge(s_idx, t + 1)
                pool.sem_inc(s_issue, 1)
                pool.indirect_dma_start(out=bufs[:, b, :], out_offset=None, in_=y_dram[:, :],
                                        in_offset=bass.IndirectOffsetOnAxis(ap=idx[:, b:b + 1], axis=0),
                                        bounds_check=NPL - 1, oob_is_err=False).then_inc(gathered[b], 16)

            def scatter(t, b):
                pool.wait_ge(s_res, (t + 1) * 8)
                pool.sem_inc(s_issue, 1)
                pool.indirect_dma_start(out=out_rows[:, :], out_offset=bass.IndirectOffsetOnAxis(ap=idx[:, b:b + 1], axis=0),
                                        in_=bufs[:, b, :], in_offset=None,
                                        bounds_check=NPL - 1, oob_is_err=False).then_inc(written[b], 16)

            def step(t, u):
                if not (isinstance(t, int) and t < 2):
                    pool.wait_ge(written[(u + 2) % BUFS], ((t - 2) // BUFS + 1) * 16 if isinstance(t, int)
                                 else turn_of(t, u - 2))
                if not (isinstance(t, int) and t + 2 >= NT):
                    gather(t + 2, (u + 2) % BUFS)
                if not (isinstance(t, int) and t < 1):
                    scatter(t - 1, (u - 1) % BUFS)

            gather(0, 0)
            gather(1, 1)
            for u in range(BUFS):
                step(u, u)
            with pool.Fori(1, NT // BUFS - 1) as g:
                def turn_of(t, back):
                    return (g + (1 if back >= 0 else 0)) * 16
                for u in range(BUFS):
                    step(g * BUFS + u, u)
            for u in range(BUFS):
                step(NT - BUFS + u, u)
            scatter(NT - 1, BUFS - 1)
            for b in range(BUFS):
                pool.wait_ge(written[b], NT // BUFS * 16)

        @block.scalar
        def _(act):
            def group_root(k):
                act.wait_ge(s_gavg, 2 * k + 2)
                act.activation(grs[:, :], psum[:, BANK_N, CT:2 * CT], ACT.Sqrt, bias=epsg[:, :]).then_inc(s_gsq, 1)

            def normalise(i, c, first=False):
                n0 = (i * CH + c) * CT
                act.wait_ge(s_newton, 3 * i + 3)
                if not first:
                    act.wait_ge(s_chunk_used, i * CH + c - RING + 1)
                for ct in range(CT):
                    if not (isinstance(n0, int) and n0 + ct < 2):
                        act.wait_ge(s_gl, n0 + ct - 1)
                    act.sem_inc(s_carry_a, 1)
                    piece = xs(ct, c * CW, CW, i % 2)
                    act.activation(g32[:, ct % 2, :], piece, ACT.Identity, bias=gbias[:, ct:ct + 1],
                                   scale=grstd[:, ct:ct + 1])
                    act.activation(gh[:, ct, (c % RING) * CW:(c % RING + 1) * CW], piece, ACT.Identity,
                                   bias=gbias[:, ct:ct + 1], scale=grstd[:, ct:ct + 1]).then_inc(s_gh, 1)

            def conv_out(i, c, o):
                n = (i * CH + c) * CT + o
                act.wait_ge(s_conv, n + 1)
                if isinstance(n, int) and n < 2:
                    pass
                else:
                    act.wait_ge(s_added, n - 1)
                act.activation(relu[:, o % 2, :], psum[:, o, :], ACT.Relu, bias=bias_sb[:, o:o + 1],
                               scale=1.0 / (SC * SC)).then_inc(s_relu, 1)

            def after(i, c):
                act.wait_ge(s_turned, i * CH + c + 1)
                half = (c % 2) * PAIRS * P
                n = (PAIRS - 1) * P if c == CH - 1 else PAIRS * P
                act.activation(bq[:, AFTER, half:half + n], psum[:, BANK_N, 0:n], ACT.Copy).then_inc(s_after, 1)

            def image(i, first, last):
                after(i, 0)
                for c in range(CH):
                    n = i * CH + c
                    act.wait_ge(s_pick, n + 1)
                    act.activation(sq[0:D, :], psum[0:D, BANK_A, :], ACT.Square).then_inc(s_sq, 1)
                    if c > 0:
                        conv_out(i, c - 1, 0)
                        conv_out(i, c - 1, 1)
                    act.wait_ge(s_norm, n + 1)
                    act.activation(sq[0:REP, :], psum[0:REP, BANK_N, :], ACT.Sqrt,
                                   bias=epsd[0:REP, :]).then_inc(s_root, 1)
                    if c > 0:
                        conv_out(i, c - 1, 2)
                        conv_out(i, c - 1, 3)
                    if c + 1 < CH:
                        after(i, c + 1)
                    if c + 3 < CH:
                        normalise(i, c + 3, first=isinstance(i, int) and i == 0 and c == 0)
                    elif not last:
                        if c + 3 == CH:
                            group_root(i + 1)
                        normalise(i + 1, c + 3 - CH)
                for o in range(CT):
                    conv_out(i, CH - 1, o)

            act.wait_ge(s_wsplit, 5)
            group_root(0)
            for c in range(3):
                normalise(0, c, first=True)
            image(0, True, False)
            if B > 2:
                with act.Fori(1, B - 1) as i:
                    image(i, False, False)
            image(B - 1, False, True)

            act.wait_ge(s_smm, 2)
            act.activation(sr, psum[:, 1, 0:NC], ACT.Sqrt, bias=epsg[:, :]).then_inc(s_sroot, 1)

            def pad_plane(t, u):
                act.wait_ge(gathered[u], turns_done(t, u))
                if not (isinstance(t, int) and t == 0):
                    act.wait_ge(s_rows, t)
                act.activation(ypad[:, :, PADC:PADC + W], bufs[:, u, :].rearrange("p (h w) -> p h w", w=W),
                               ACT.Copy).then_inc(s_ypad, 1)

            def diagonals(t, s):
                if not (isinstance(t, int) and t < 2):
                    act.wait_ge(s_res, (t - 1) * 8)
                    act.wait_ge(s_rec, 16)
                for k in range(3):
                    act.activation(diag[:, s, k, :], ident, ACT.Copy, scale=rec_sb[:, bass.ds(t, 1), 1 + k])
                act.activation(const_t[:, s:s + 1], rec_sb[:, bass.ds(t, 1), 4], ACT.Copy).then_inc(s_diag, 1)

            def results(t, u):
                act.wait_ge(s_diag, t + 1)
                for b in range(8):
                    act.wait_ge(s_mix, t * 8 + b + 1)
                    act.activation(bufs[:, u, b * CW:(b + 1) * CW], psum[:, b, :], ACT.Identity,
                                   bias=const_t[:, u % 2:u % 2 + 1]).then_inc(s_res, 1)

            def turns_done(t, u):
                return (t // BUFS + 1) * 16 if isinstance(t, int) else turns[0](t, u)

            turns = [None]

            def step(t, u):
                if not (isinstance(t, int) and t + 1 >= NT):
                    pad_plane(t + 1, (u + 1) % BUFS)
                if not (isinstance(t, int) and t == 0):
                    results(t - 1, (u - 1) % BUFS)
                if not (isinstance(t, int) and t + 1 >= NT):
                    diagonals(t + 1, (u + 1) % 2)

            act.wait_ge(s_pads, 1)
            act.wait_ge(s_rec, 16)
            pad_plane(0, 0)
            diagonals(0, 0)
            for u in range(BUFS):
                step(u, u)
            with act.Fori(1, NT // BUFS - 1) as g:
                turns[0] = lambda t, u: (g + (2 if u == 0 else 1)) * 16
                for u in range(BUFS):
                    step(g * BUFS + u, u)
            for u in range(BUFS):
                step(NT - BUFS + u, u)
            results(NT - 1, BUFS - 1)

        @block.vector
        def _(dve):
            chain = [0]

            def split_weights():
                dve.memset(epsd[:, :], EPS_D * SC * SC)
                dve.memset(epsg[:, :], EPS)
                dve.wait_ge(s_const, 48)
                dve.tensor_scalar(stage_w, stage_w, SC, None, ALU.mult).then_inc(s_wsplit, 1)
                dve.wait_ge(s_wd_in, 48)
                dve.tensor_scalar(stage_d, stage_d, SC, None, ALU.mult).then_inc(s_wsplit, 1)
                dve.wait_ge(s_wsplit, 2)
                dve.tensor_copy(wh, stage_w)
                dve.tensor_copy(wd, stage_d).then_inc(s_wsplit, 1)
                dve.wait_ge(s_wsplit, 3)
                dve.tensor_tensor(wl, stage_w, wh, ALU.subtract).then_inc(s_wsplit, 1)
                dve.tensor_tensor(wd[32:64, :], stage_d[32:64, :], wd[32:64, :], ALU.subtract).then_inc(s_wsplit, 1)

            def x_stats(i, q):
                dve.wait_ge(x_loaded[q], (i + 1) * 16)
                for ct in range(CT):
                    for c in (2 * q, 2 * q + 1):
                        last = dve.bn_stats(bnx[:, ct, c, :], xs(ct, c * CW, CW, i % 2))
                if q == 3:
                    last.then_inc(s_vchain, 1)

            def group_stats(i):
                b = i * STATS_CHAIN
                dve.wait_ge(s_vchain, b + 1)
                dve.sem_inc(s_carry, 1)
                for ct in range(CT):
                    last = dve.bn_aggr(aggx[:, ct, :], bnx[:, ct, :, :].rearrange("p c s -> p (c s)"))
                last.then_inc(s_xagg, 1)
                dve.wait_ge(s_xagg, 2 * i + 1)
                dve.wait_ge(s_gavg, 2 * i + 1)
                dve.tensor_copy(gm[:, :], psum[:, BANK_N, 0:CT]).then_inc(s_vchain, 1)
                dve.wait_ge(s_vchain, b + 2)
                dve.tensor_tensor(gd[:, :], aggx[:, :, 0], gm[:, :], ALU.subtract).then_inc(s_vchain, 1)
                dve.wait_ge(s_vchain, b + 3)
                dve.tensor_tensor(gd[:, :], gd[:, :], gd[:, :], ALU.mult).then_inc(s_vchain, 1)
                dve.wait_ge(s_vchain, b + 4)
                dve.tensor_tensor(gd[:, :], gd[:, :], aggx[:, :, 1], ALU.add).then_inc(s_xagg, 1)
                dve.wait_ge(s_gsq, i + 1)
                dve.reciprocal(gd[:, :], grs[:, :]).then_inc(s_vchain, 1)
                dve.wait_ge(s_vchain, b + 5)
                dve.tensor_tensor(grs[:, :], gd[:, :], gd[:, :], ALU.mult).then_inc(s_vchain, 1)
                dve.wait_ge(s_vchain, b + 6)
                dve.scalar_tensor_tensor(grs[:, :], psum[:, BANK_N, CT:2 * CT], EPS, grs[:, :],
                                         ALU.add, ALU.mult).then_inc(s_vchain, 1)
                dve.wait_ge(s_vchain, b + 7)
                dve.tensor_scalar(grs[:, :], grs[:, :], -0.5 * SC, 1.5 * SC, ALU.mult, ALU.add).then_inc(s_newton, 1)
                dve.wait_ge(s_newton, 3 * i + 1)
                dve.tensor_tensor(grstd[:, :], grs[:, :], gd[:, :], ALU.mult).then_inc(s_newton, 1)
                dve.wait_ge(s_newton, 3 * i + 2)
                dve.scalar_tensor_tensor(gbias[:, :], gm[:, :], -1.0, grstd[:, :], ALU.mult, ALU.mult)\
                    .then_inc(s_newton, 1)

            def low_parts(i, c):
                n0 = (i * CH + c) * CT
                slot = slice((c % RING) * CW, (c % RING + 1) * CW)
                for ct in range(CT):
                    dve.wait_ge(s_gh, n0 + ct + 1)
                    dve.tensor_tensor(gl[:, ct, slot], g32[:, ct % 2, :], gh[:, ct, slot],
                                      ALU.subtract).then_inc(s_gl, 1)

            def mask(i, t):
                dve.wait_ge(s_gram, i * NB + t + 1)
                bank = GRAM0 + t % 2
                same, before_ = (t % PRING) * P, ((t + 1) % PRING) * P
                if t + 1 < NB and before_:
                    base = bq_off + SAME * PRING * P + same
                    dst = arena[:, base:base + 2 * (PRING + 1) * P]\
                        .rearrange("p (r n) -> p r n", r=2)[:, :, 0:P]
                    dve.tensor_tensor(dst, psum[:, bank, 0:2 * P].rearrange("p (r n) -> p r n", r=2),
                                      band.unsqueeze(1).to_broadcast([P, 2, P]), ALU.mult).then_inc(s_masked, 1)
                    return
                if t + 1 < NB:
                    dve.tensor_tensor(bq[:, BEFORE, before_:before_ + P], psum[:, bank, P:2 * P], band, ALU.mult)
                dve.tensor_tensor(bq[:, SAME, same:same + P], psum[:, bank, 0:P], band, ALU.mult).then_inc(s_masked, 1)

            def residual(i, c, o):
                n = (i * CH + c) * CT + o
                y = xs(o, c * CW, CW, i % 2)
                dve.wait_ge(s_relu, n + 1)
                dve.tensor_tensor(y, y, relu[:, o % 2, :], ALU.add).then_inc(s_added, 1)
                dve.wait_ge(s_added, n + 1)
                dve.bn_stats(bny[:, o, c, :], y).then_inc(s_y, 1)

            def descriptor(i, c):
                n = i * CH + c
                dve.wait_ge(s_root, n + 1)
                dve.reciprocal(sq[0:REP, :], sq[0:REP, :]).then_inc(s_rinv, 1)
                dve.wait_ge(s_rinv, n + 1)
                if not (isinstance(n, int) and n == 0):
                    dve.wait_ge(s_t, n)
                dve.tensor_tensor(fn[0:REP, :], psum[0:REP, BANK_A, :], sq[0:REP, :], ALU.mult).then_inc(s_fn, 1)

            def masks_of(i, c, between):
                if c == 0:
                    if not (isinstance(i, int) and i == 0):
                        dve.wait_ge(s_pick, i * CH)
                else:
                    dve.wait_ge(s_pick, i * CH + c)
                for k in range(PAIRS):
                    mask(i, PAIRS * c + k)
                    if between:
                        between[k]()

            def image(i, last):
                masks_of(i, 0, [])
                for c in range(CH):
                    res = [lambda o=o: residual(i, c - 1, o) for o in range(CT)] if c > 0 else []
                    if c + 1 < CH:
                        masks_of(i, c + 1, res)
                    else:
                        for f in res:
                            f()
                    descriptor(i, c)
                    if c + 3 < CH:
                        low_parts(i, c + 3)
                    elif not last:
                        if c + 3 == CH:
                            group_stats(i + 1)
                        low_parts(i + 1, c + 3 - CH)
                    if 1 <= c <= 4 and not last:
                        x_stats(i + 1, c - 1)
                for o in range(CT):
                    residual(i, CH - 1, o)
                dve.wait_ge(s_y, (i + 1) * CH * CT)
                dve.sem_inc(s_carry, 1)
                for ct in range(CT):
                    ins = dve.bn_aggr(aggy[:, ct, :], bny[:, ct, :, :].rearrange("p c s -> p (c s)"))
                ins.then_inc(s_yagg, 1)
                dve.wait_ge(s_yagg, i + 1)
                dve.tensor_copy(ymv[:, bass.ds(i * (2 * CT), 2 * CT)],
                                aggy[:, :, :].rearrange("p t s -> p (t s)")).then_inc(s_ymv, 1)

            def sort_planes():
                links = [0]

                def link(ins):
                    links[0] += 1
                    ins.then_inc(s_link, 1)
                    dve.wait_ge(s_link, links[0])

                stats = ymv[:, :].rearrange("p (n s) -> p n s", s=2)
                dve.wait_ge(s_ymv, B)
                dve.wait_ge(s_conv, B * CH * CT)
                dve.memset(zeros, 0.0)
                dve.tensor_copy(sm, stats[:, :, 0]).then_inc(s_sstat, 1)
                dve.wait_ge(s_smm, 1)
                link(dve.tensor_tensor(sd, sm, psum[:, 0, 0:NC], ALU.subtract))
                link(dve.tensor_tensor(tmp, sd, sd, ALU.mult))
                dve.tensor_tensor(tmp, tmp, stats[:, :, 1], ALU.add).then_inc(s_sstat, 1)
                dve.wait_ge(s_sroot, 1)
                link(dve.reciprocal(sa, sr))
                link(dve.tensor_tensor(sr, sa, sa, ALU.mult))
                link(dve.scalar_tensor_tensor(sr, psum[:, 1, 0:NC], EPS, sr, ALU.add, ALU.mult))
                link(dve.tensor_scalar(sr, sr, -0.5, 1.5, ALU.mult, ALU.add))
                link(dve.tensor_tensor(sa, sr, sa, ALU.mult))
                link(dve.scalar_tensor_tensor(scc, psum[:, 0, 0:NC], -1.0, sa, ALU.mult, ALU.mult))
                dve.tensor_tensor(sgap, sd, sa, ALU.mult).then_inc(s_sstat, 1)
                dve.wait_ge(s_w12, 64)
                dve.wait_ge(s_smm, 3)
                dve.tensor_scalar(hid[0:HID, :], psum[0:HID, 2, 0:B], b1_sb[0:HID, :], 0.0, ALU.add, ALU.max)\
                    .then_inc(s_sstat, 1)
                dve.wait_ge(s_smm, 4)
                link(dve.tensor_tensor(score.rearrange("p (b t) -> p b t", t=CT),
                                       psum[:, 3, 0:NC].rearrange("p (t b) -> p b t", t=CT),
                                       b2_sb.unsqueeze(1).to_broadcast([P, B, CT]), ALU.add))
                link(dve.tensor_scalar(score, score, 0.0, None, ALU.max))
                link(dve.tensor_scalar(cls, score, 1.0, None, ALU.is_ge))
                for k in range(2, NCLS):
                    link(dve.scalar_tensor_tensor(cls, score, float(k), cls, ALU.is_ge, ALU.add))
                for k in range(NCLS):
                    ins = dve.tensor_scalar(onehot[:, k * NC:(k + 1) * NC], cls, float(k), None, ALU.is_equal)
                ins.then_inc(s_sstat, 1)
                link(dve.scalar_tensor_tensor(fs, cls, 1.0, score, ALU.add, ALU.subtract))
                link(dve.tensor_tensor(fb, score, cls, ALU.subtract))
                dve.wait_ge(s_iota, 2)
                dve.tensor_scalar(recs[:, :, 1], sa, 1.0, None, ALU.add)
                dve.tensor_tensor(recs[:, :, 2], fs, sa, ALU.mult)
                dve.tensor_tensor(recs[:, :, 3], fb, sa, ALU.mult)
                link(dve.scalar_tensor_tensor(tmp, fs, 1.0, fb, ALU.add, ALU.add))
                dve.tensor_tensor(recs[:, :, 4], tmp, scc, ALU.mult)
                dve.memset(recs[:, :, 5:REC], 0.0)
                dve.wait_ge(s_smm, 6)
                for k in range(NCLS):
                    cols = slice(k * NC, (k + 1) * NC)
                    ins = dve.tensor_tensor_scan(incl[:, cols], psum[:, 5, cols], zeros, 0.0, ALU.add, ALU.add)
                link(ins)
                link(dve.tensor_tensor(rank, incl, psum[:, 5, 0:NCLS * NC], ALU.subtract))
                link(dve.tensor_tensor(rank, rank, psum[:, 4, 0:NCLS * NC], ALU.add))
                totals = incl.rearrange("p (k n) -> p k n", k=NCLS)[:, :, NC - 1]
                link(dve.tensor_scalar(tiles, totals, 1.0 / P, 0.5 - 0.5 / P, ALU.mult, ALU.add))
                link(dve.tensor_scalar(tiles, tiles, 2.0 ** 23, None, ALU.add))
                link(dve.tensor_scalar(tiles, tiles, -2.0 ** 23, None, ALU.add))
                link(dve.tensor_tensor_scan(tincl, tiles, zeros[:, 0:NCLS], 0.0, ALU.add, ALU.add))
                link(dve.tensor_tensor(tbase, tincl, tiles, ALU.subtract))
                link(dve.tensor_scalar(tb128, tbase, float(P), None, ALU.mult))
                for k in range(NCLS):
                    cols = slice(k * NC, (k + 1) * NC)
                    ins = dve.scalar_tensor_tensor(rank[:, cols], rank[:, cols], tb128[:, k:k + 1], onehot[:, cols],
                                                   ALU.add, ALU.mult)
                link(ins)
                link(dve.tensor_reduce(slot_f, rank.rearrange("p (k n) -> p n k", k=NCLS), AX.X, ALU.add))
                dve.tensor_copy(slot_i, slot_f)
                link(dve.tensor_copy(tnum, tnum_i))
                link(dve.tensor_scalar(tcls, tnum, tincl[:, 0:1], None, ALU.is_ge))
                for k in range(1, NCLS):
                    link(dve.scalar_tensor_tensor(tcls, tnum, tincl[:, k:k + 1], tcls, ALU.is_ge, ALU.add))
                dve.tensor_copy(cls_i, tcls).then_inc(s_sorted, 1)

            OWN = 20

            def pools(t, s, k):
                used = [0]

                def op(dst, a, b, wait=True, signal=s_own):
                    if wait and used[0]:
                        dve.wait_ge(s_own, t * OWN + used[0])
                    ins = dve.tensor_tensor(dst, a, b, ALU.max)
                    ins.then_inc(signal, 1)
                    if signal is s_own:
                        used[0] += 1

                def window(src, mid, dst, r, signal=s_own):
                    m, w = half_m, half_w
                    n = 31 + r
                    op(mid(m, 0, n), src(1 - r, n), src(2 - r, n))
                    core = m
                    if r >= 2:
                        op(mid(w, 0, n - 1), mid(m, 0, n - 1), mid(m, 1, n - 1))
                        core = w
                    if r == 3:
                        op(mid(m, 0, 32), mid(w, 0, 32), mid(w, 1, 32))
                        core = m
                    if r >= 4:
                        op(mid(m, 0, 32), mid(w, 0, 32), mid(w, 2, 32))
                        core = m
                    if r == 5:
                        op(mid(m, 0, 32), mid(m, 0, 32), mid(w, 3, 32))
                    op(dst(0), mid(core, 0, 32), src(-r, 32))
                    op(dst(1), mid(core, 0, 32), src(1 + r, 32), wait=False, signal=signal)

                def cols(i, n):
                    return ypad[:, :, PADC + i:PADC + i + 2 * n - 1:2]

                def cols_mid(a, i, n):
                    return a.rearrange("p (h w) -> p h w", w=36)[:, :, i:i + n]

                def rows(i, n):
                    return hbuf[:, PADC + i:PADC + i + 2 * n - 1:2, :]

                def rows_mid(a, i, n):
                    return a.rearrange("p (h w) -> p h w", w=W)[:, i:i + n, :]

                sm_, bg = small[:, s, :, :], big[:, s, :].rearrange("p (h w) -> p h w", w=W)
                inner = hbuf[:, PADC:PADC + H, :]
                if k == 0:
                    window(cols, cols_mid, lambda e: inner[:, :, e::2], 1)
                    dve.tensor_copy(sm_[:, :, 1:W + 1], ypad[:, :, PADC:PADC + W]).then_inc(s_rows, 1)
                    window(rows, rows_mid, lambda e: bg[:, e::2, :], 1, signal=s_pool)
                else:
                    window(cols, cols_mid, lambda e: inner[:, :, e::2], k, signal=s_rows)
                    dve.wait_ge(s_rows, t + 1)
                    window(rows, rows_mid, lambda e: sm_[:, e::2, 1:W + 1], k)
                    op(inner, sm_[:, :, 0:W], sm_[:, :, 2:W + 2])
                    op(bg, hbuf[:, PADC - 1:PADC - 1 + H, :], hbuf[:, PADC + 1:PADC + 1 + H, :], signal=s_pool)
                assert used[0] <= OWN
                dve.sem_inc(s_own, OWN - used[0])

            def tile(t, s):
                cls_t = dve.value_load(cls_i[0:1, bass.ds(t, 1)], min_val=0, max_val=NCLS)

                def waits():
                    dve.wait_ge(s_ypad, t + 1)
                    if not (isinstance(t, int) and t < 2):
                        dve.wait_ge(s_mix, (t - 1) * 8)
                    if not (isinstance(t, int) and t == 0):
                        dve.wait_ge(s_pool, t)

                def branch(lo, hi):
                    if lo == hi:
                        waits()
                        if lo == NCLS:
                            dve.sem_inc(s_own, OWN)
                            dve.sem_inc(s_rows, 1)
                            dve.sem_inc(s_pool, 1)
                        else:
                            pools(t, s, lo)
                        return
                    mid = (lo + hi) // 2
                    with dve.If(cls_t < mid + 1):
                        branch(lo, mid)
                    with dve.Else():
                        branch(mid + 1, hi)

                branch(0, NCLS)

            split_weights()
            for q in range(4):
                x_stats(0, q)
            group_stats(0)
            for c in range(3):
                low_parts(0, c)
            image(0, False)
            if B > 2:
                with dve.Fori(1, B - 1) as i:
                    image(i, False)
            image(B - 1, True)
            sort_planes()
            dve.wait_ge(s_pads, 1)
            for t in range(2):
                tile(t, t)
            with dve.Fori(1, NT // 2) as g:
                for s in range(2):
                    tile(g * 2 + s, s)

        @block.tensor
        def _(pe):
            def product(dst, w, m, k, nk):
                return pe.matmul(dst, w, m, start=(k == 0), stop=(k == nk - 1))

            def gram(i, t):
                if not (isinstance(i, int) and i == 0 and t < 2):
                    pe.wait_ge(s_masked, i * NB + t - 1)
                own = ((2 * t) % (RING * ROWS)) * W
                for col, ring, n in gram_parts(t):
                    for ct in range(CT):
                        sh, sl = gh[:, ct, own:own + 2 * W], gl[:, ct, own:own + 2 * W]
                        mh, ml = gh[:, ct, ring:ring + n], gl[:, ct, ring:ring + n]
                        dst = psum[:, GRAM0 + t % 2, col:col + n]
                        product(dst, sh, mh, 3 * ct, 3 * CT)
                        product(dst, sh, ml, 3 * ct + 1, 3 * CT)
                        last = product(dst, sl, mh, 3 * ct + 2, 3 * CT)
                last.then_inc(s_gram, 1)

            def conv(i, c, o):
                if not (isinstance(i, int) and i == 0 and c == 0):
                    pe.wait_ge(s_relu, (i * CH + c - 1) * CT + o + 1)
                slot = slice((c % RING) * CW, (c % RING + 1) * CW)
                for ct in range(CT):
                    h, l = wh[:, ct, o * P:(o + 1) * P], wl[:, ct, o * P:(o + 1) * P]
                    dst = psum[:, o, :]
                    pe.matmul(dst, h, gh[:, ct, slot], start=(ct == 0), stop=False)
                    pe.matmul(dst, h, gl[:, ct, slot], start=False, stop=False)
                    last = pe.matmul(dst, l, gh[:, ct, slot], start=False, stop=(ct == CT - 1))
                if o == CT - 1:
                    last.then_inc(s_chunk_used, 1)

            def picks(i, c):
                pe.wait_ge(s_after, i * CH + c + 1)
                if not (isinstance(i, int) and i == 0 and c == 0):
                    pe.wait_ge(s_fn, i * CH + c)
                dst = psum[0:REP, BANK_A, :].rearrange("p (u e w) -> p u e w", e=2, w=W)
                src = bq[:, :, (c % 2) * PAIRS * P:(c % 2 + 1) * PAIRS * P]\
                    .rearrange("p r (u e w) -> p r u e w", e=2, w=W)
                for e in range(2):
                    for k, role in enumerate((BEFORE, AFTER, SAME)):
                        u0 = 1 if role == BEFORE and c == 0 else 0
                        u1 = PAIRS - 1 if role == AFTER and c == CH - 1 else PAIRS
                        last = pe.matmul(dst[:, u0:u1, e, :], pick[:, role, e, :], src[:, role, u0:u1, e, :],
                                         start=(e == 0 and k == 0), stop=True, skip_group_check=True)
                last.then_inc(s_pick, 1)

            def turn_blocks(i, c):
                pe.wait_ge(s_masked, i * NB + PAIRS * (c + 1))
                if isinstance(i, int) and i == 0 and c == 0:
                    pe.wait_ge(s_vchain, STATS_CHAIN)
                else:
                    pe.wait_ge(s_root, i * CH + c)
                for t in range(PAIRS * c, min(PAIRS * (c + 1), NB - 1)):
                    last = pe.transpose(psum[:, BANK_N, (t % PAIRS) * P:(t % PAIRS + 1) * P],
                                        bq[:, BEFORE, ((t + 1) % PRING) * P:((t + 1) % PRING + 1) * P], ident)
                last.then_inc(s_turned, 1)

            def norm(i, c, last):
                pe.wait_ge(s_sq, i * CH + c + 1)
                if c == 6 and not last:
                    pe.wait_ge(s_vchain, (i + 2) * STATS_CHAIN)
                pe.matmul(psum[0:REP, BANK_N, :], ssum[0:D, :], sq[0:D, :], start=True, stop=True)\
                  .then_inc(s_norm, 1)

            def tail(i, c):
                pe.wait_ge(s_t, i * CH + c + 1)
                src = tpair[0:REP, c % 2, :].rearrange("p (r w) -> p r w", w=W)
                for o in range(CT):
                    dst = psum[:, o, :].rearrange("p (r w) -> p r w", w=W)
                    for k in range(KS):
                        last = pe.matmul(dst[:, :, k::KS], wd[0:REP, k * C + o * P:k * C + (o + 1) * P],
                                         src[:, :, k::KS], start=False, stop=True, skip_group_check=True)
                    last.then_inc(s_conv, 1)

            def group_average(i):
                pe.wait_ge(s_xagg, 2 * i + 1)
                if not (isinstance(i, int) and i == 0):
                    pe.wait_ge(s_after, i * CH - 1)
                pe.matmul(psum[:, BANK_N, 0:CT], gavg, aggx[:, :, 0], start=True, stop=True).then_inc(s_gavg, 1)

            def group_spread(i):
                pe.wait_ge(s_xagg, 2 * i + 2)
                pe.matmul(psum[:, BANK_N, CT:2 * CT], gavg, gd[:, :], start=True, stop=True).then_inc(s_gavg, 1)

            def image(i, last):
                pe.wait_ge(s_gl, (i * CH + 2) * CT)
                for t in range(PAIRS):
                    gram(i, t)
                conv(i, 0, 0)
                turn_blocks(i, 0)
                conv(i, 0, 1)
                for c in range(CH):
                    convs = list(range(2 if c == 0 else 0, CT))
                    picks(i, c)
                    if c + 1 < CH:
                        pe.wait_ge(s_gl, (i * CH + min(c + 3, CH)) * CT)
                        gram(i, PAIRS * (c + 1))
                        gram(i, PAIRS * (c + 1) + 1)
                    else:
                        conv(i, c, convs.pop(0))
                    norm(i, c, last)
                    if c + 1 < CH:
                        gram(i, PAIRS * (c + 1) + 2)
                        gram(i, PAIRS * (c + 1) + 3)
                        conv(i, c, convs.pop(0))
                        turn_blocks(i, c + 1)
                    for n, o in enumerate(convs):
                        conv(i, c, o)
                        if c == 5 and not last and n == 0:
                            group_average(i + 1)
                        if c == 5 and not last and n == 1:
                            group_spread(i + 1)
                    tail(i, c)

            pe.wait_ge(s_wsplit, 5)
            group_average(0)
            group_spread(0)
            image(0, False)
            if B > 2:
                with pe.Fori(1, B - 1) as i:
                    image(i, False)
            image(B - 1, True)

            stats = ymv[:, :].rearrange("p (n s) -> p n s", s=2)
            pe.wait_ge(s_relu, B * CH * CT)
            pe.wait_ge(s_sstat, 1)
            pe.matmul(psum[:, 0, 0:NC], gavg, sm, start=True, stop=True).then_inc(s_smm, 1)
            pe.wait_ge(s_sstat, 2)
            pe.matmul(psum[:, 1, 0:NC], gavg, tmp, start=True, stop=True).then_inc(s_smm, 1)
            pe.wait_ge(s_sstat, 3)
            pe.wait_ge(s_w12, 64)
            gap = sgap.rearrange("p (b t) -> p b t", t=CT)
            for ct in range(CT):
                last = product(psum[0:HID, 2, 0:B], w1_sb[:, ct, :], gap[:, :, ct], ct, CT)
            last.then_inc(s_smm, 1)
            pe.wait_ge(s_sstat, 4)
            for ct in range(CT):
                last = pe.matmul(psum[:, 3, ct * B:(ct + 1) * B], w2_sb[0:HID, ct * P:(ct + 1) * P], hid[0:HID, :],
                                 start=True, stop=True)
            last.then_inc(s_smm, 1)
            pe.wait_ge(s_sstat, 5)
            pe.matmul(psum[:, 4, 0:NCLS * NC], before, onehot, start=True, stop=True).then_inc(s_smm, 1)
            pe.matmul(psum[:, 5, 0:NCLS * NC], ones, onehot, start=True, stop=True).then_inc(s_smm, 1)

            def mix(t, u):
                s = u % 2
                pe.wait_ge(s_diag, t + 1)
                pe.wait_ge(s_pool, t + 1)
                for b in range(8):
                    if not (isinstance(t, int) and t == 0):
                        pe.wait_ge(s_res, (t - 1) * 8 + b + 1)
                    dst = psum[:, b, :]
                    pe.matmul(dst, diag[:, s, 0, :], bufs[:, u, b * CW:(b + 1) * CW], start=True, stop=False)
                    pe.matmul(dst, diag[:, s, 1, :], small[:, s, b * ROWS:(b + 1) * ROWS, 1:W + 1],
                              start=False, stop=False)
                    pe.matmul(dst, diag[:, s, 2, :], big[:, s, b * CW:(b + 1) * CW], start=False, stop=True)\
                      .then_inc(s_mix, 1)

            pe.wait_ge(s_sorted, 1)
            for u in range(BUFS):
                mix(u, u)
            with pe.Fori(1, NT // BUFS) as g:
                for u in range(BUFS):
                    mix(g * BUFS + u, u)


def kernel(x, L0_conv_W, L0_conv_bias, L1_conv_w1, L1_conv_b1, L1_conv_w2, L1_conv_b2):
    import concourse.bacc as _bacc
    from concourse.bass_utils import run_bass_kernel_spmd as _run

    nc = _bacc.Bacc("TRN2", target_bir_lowering=False, num_devices=1)
    ins = {
        "x": x, "wt": L0_conv_W[:, :C].T, "wturn": L0_conv_W.T[turned_rows()].reshape(D, KS * C), "bias": L0_conv_bias, "w1t": L1_conv_w1.T, "b1": L1_conv_b1,
        "w2t": L1_conv_w2.T, "b2": L1_conv_b2, "consts": const_arrays(),
    }
    arrays, args = {}, []
    for name, a in ins.items():
        a = np.ascontiguousarray(a)
        arrays[f"in_{name}"] = a
        args.append(nc.dram_tensor(f"in_{name}", a.shape, mybir.dt.from_np(a.dtype), kind="ExternalInput").ap())
    out = nc.dram_tensor("out", x.shape, mybir.dt.float32, kind="ExternalOutput").ap()
    build(nc, *args, out)
    r = _run(nc, [arrays], core_ids=[0])
    return r.results[0]["out"]
```

```python
import numpy as np
from contextlib import ExitStack

import concourse.bass as bass
from concourse import mybir

P = 128
C, H, W = 512, 64, 64
PIX = H * W
CT = C // P
ROWS = 8
CH = H // ROWS
CW = ROWS * W
NB = H // 2
PAIRS = ROWS // 2
PRING = 2 * PAIRS
AFTER, SAME, BEFORE = range(3)
KS = 5
D = KS * KS
CG = 16
HID = 32
NCLS = 6
SC = 64.0
EPS = 1e-5
EPS_D = 1e-6
RING = 4
LOWEST = -3.4028234663852886e38
PADC = 6
REC = 4
MAGIC = 1.5 * 2.0 ** 23
BUFS = 4
REP = 3 * 32


def const_arrays():
    p = np.arange(P)
    r, w = p // W, p % W
    q = np.arange(2 * W)
    band = (np.abs(w[:, None] - (q % W)[None, :]) <= KS // 2).astype(np.float32)
    pick = np.zeros((P, 3, 2, REP), np.float32)
    for role in range(3):
        for e in range(2):
            di = r + 2 * (1 - role) - e
            ok = np.abs(di) <= KS // 2
            for rep in range(3):
                pick[p[ok], role, e, (32 * rep + (di + 2) * KS + w % KS)[ok]] = 1.0
    ssum = np.zeros((P, REP), np.float32)
    ssum[:D] = 2.0 ** -12
    gavg = (p[:, None] // CG == p[None, :] // CG).astype(np.float32) / CG
    ident = np.eye(P, dtype=np.float32)
    before = (p[:, None] < p[None, :]).astype(np.float32)
    ones = np.ones((P, P), np.float32)
    return np.concatenate([band, pick.reshape(P, -1), ssum, gavg, ident, before, ones], axis=1)


CONST_W = 2 * W + 3 * 2 * REP + REP + 4 * P


def turned_rows():
    rows = np.zeros((D, KS), np.int64)
    for k in range(KS):
        for di in range(KS):
            for dj in range(-2, 3):
                rows[di * KS + (k + dj) % KS, k] = C + di * KS + dj + 2
    return rows


def build(nc, x, wt, wturn, bias, w1t, b1, w2t, b2, consts, out):
    fp32, fp16, i32 = mybir.dt.float32, mybir.dt.float16, mybir.dt.int32
    ALU, ACT, AX = mybir.AluOpType, mybir.ActivationFunctionType, mybir.AxisListType
    B = x.shape[0]
    NC = B * CT
    NPL = NC * P
    NT = -(-(NC + NCLS - 1) // BUFS) * BUFS
    COLS = min(8, NC // 2)
    assert B >= 2 and NC % (2 * COLS) == 0
    nc.disable_value_cache = True

    x_v = x.rearrange("b (t p) h w -> b p t (h w)", p=P)
    out_rows = out.rearrange("b c h w -> (b c) (h w)")
    y_dram = nc.dram_tensor("y_planes", [NPL, PIX], fp32, kind="Internal").ap()
    y_v = y_dram.rearrange("(b t p) n -> b p t n", t=CT, p=P)
    no_out = nc.dram_tensor("no_out", [NT, REC], fp32, kind="Internal").ap()
    rec_dram = nc.dram_tensor("plane_records", [NPL, REC], fp32, kind="Internal").ap()

    ctx = ExitStack()
    with ctx:
        def sem(name):
            return ctx.enter_context(nc.semaphore(name))

        def sb(name, shape, dt):
            return ctx.enter_context(nc.sbuf_tensor(name, shape, dt))

        cst = sb("cst", [P, CONST_W], fp32)
        o = 0
        band = cst[:, o:o + 2 * W]; o += 2 * W
        pick = cst[:, o:o + 6 * REP].rearrange("p (r e m) -> p r e m", r=3, e=2); o += 6 * REP
        ssum = cst[:, o:o + REP]; o += REP
        gavg = cst[:, o:o + P]; o += P
        ident = cst[:, o:o + P]; o += P
        before = cst[:, o:o + P]; o += P
        ones = cst[:, o:o + P]; o += P
        bias_sb = sb("bias_sb", [P, CT], fp32)
        epsd = sb("epsd", [P, 1], fp32)
        epsg = sb("epsg", [P, 1], fp32)
        bnx = sb("bnx", [P, CT, CH, 6], fp32)
        bny = sb("bny", [P, CT, CH, 6], fp32)
        aggx = sb("aggx", [P, CT, 2], fp32)
        aggy = sb("aggy", [P, CT, 2], fp32)
        ymv = sb("ymv", [P, B * CT * 2], fp32)
        gm = sb("gm", [P, CT], fp32)
        gd = sb("gd", [P, CT], fp32)
        grs = sb("grs", [P, CT], fp32)
        gbias = sb("gbias", [P, CT], fp32)
        grstd = sb("grstd", [P, CT], fp32)

        ARENA = 50944
        arena = sb("arena", [P, ARENA], fp32)
        pos = [0]

        def take(n):
            pos[0] += n
            assert pos[0] <= ARENA
            return arena[:, pos[0] - n:pos[0]]

        take(2 * CT * PIX)
        gh = take(CT * RING * CW // 2).bitcast(fp16).rearrange("p (t n) -> p t n", t=CT)
        gl = take(CT * RING * CW // 2).bitcast(fp16).rearrange("p (t n) -> p t n", t=CT)
        g32 = take(2 * CW).rearrange("p (s n) -> p s n", s=2)
        bq_off = pos[0]
        bq = take(3 * PRING * P).rearrange("p (r n) -> p r n", r=3)
        sq = take(CW)
        fn = take(CW)
        tpair = take(CW).bitcast(fp16).rearrange("p (s n) -> p s n", s=2)
        relu = take(2 * CW).rearrange("p (s n) -> p s n", s=2)
        wh = take(CT * C // 2).bitcast(fp16).rearrange("p (t n) -> p t n", t=CT)
        wl = take(CT * C // 2).bitcast(fp16).rearrange("p (t n) -> p t n", t=CT)
        wd = take(KS * C // 2).bitcast(fp16)
        stage_w = arena[:, CT * PIX:CT * PIX + CT * C].rearrange("p (t n) -> p t n", t=CT)
        stage_d = arena[:, CT * PIX + CT * C:CT * PIX + (CT + KS) * C]


        def xs_quarter(par, q):
            return arena[:, bass.ds(par * (CT * PIX), CT * PIX)]\
                .rearrange("p (t n) -> p t n", t=CT)[:, :, q * (PIX // 4):(q + 1) * (PIX // 4)]

        v = lambda n: take(n)
        pos[0] = (B - 2) % 2 * CT * PIX
        w1_sb = v(CT * HID).rearrange("p (t e) -> p t e", t=CT)
        w2_sb = v(C)
        b1_sb = v(1)
        b2_sb = v(CT)
        pos[0] = 2 * CT * PIX
        sm, sd, sa, sr, scc, sgap = (v(NC) for _ in range(6))
        score, cls, fs, fb, tmp = (v(NC) for _ in range(5))
        hid = v(B)
        onehot = v(NCLS * NC)
        incl = v(NCLS * NC)
        rank = v(NCLS * NC)
        zeros = v(NC)
        tiles, tincl, tbase, tb128 = (v(NCLS) for _ in range(4))
        slot, slot_hi, slot_lo = (v(NC) for _ in range(3))
        plane_i = v(NC).bitcast(i32)
        plane_f = v(NC)
        lane_i = v(P).bitcast(i32)
        lane = v(P)
        at_lane = v(2 * COLS * P).rearrange("p (s j n) -> p s j n", s=2, j=COLS)
        at_tile = v(2 * COLS * NT).rearrange("p (s j n) -> p s j n", s=2, j=COLS)
        empty = v(NT)
        tnum_i = v(NT).bitcast(i32)
        tnum = v(NT)
        tcls = v(NT)
        recs = v(NC * REC).rearrange("p (n e) -> p n e", e=REC)
        assert pos[0] <= 2 * CT * PIX + CT * RING * CW
        pos[0] = 0
        bufs = v(BUFS * PIX).rearrange("p (b n) -> p b n", b=BUFS)
        WP = W + 2 * PADC
        ypad_f = v(H * WP)
        ypad = ypad_f.rearrange("p (h w) -> p h w", w=WP)
        hbuf_f = v((H + 2 * PADC) * W)
        hbuf = hbuf_f.rearrange("p (h w) -> p h w", w=W)
        small_f = v(2 * H * (W + 2))
        small = small_f.rearrange("p (s h w) -> p s h w", s=2, h=H)
        big = v(2 * PIX).rearrange("p (s n) -> p s n", s=2)
        half_m, half_w = v(36 * W), v(36 * W)
        ids = v(NT)
        ids_i = v(NT).bitcast(i32)
        recs_in = v(BUFS * REC).rearrange("p (b e) -> p b e", e=REC)
        diag = v(2 * 3 * P).rearrange("p (s k n) -> p s k n", s=2, k=3)
        cls_i = v(NT).bitcast(i32)
        idx = v(BUFS).bitcast(i32)
        const_t = v(2)

        psum = ctx.enter_context(nc.psum_tensor("psum", [P, 8, 512], fp32))
        GRAM0, BANK_A, BANK_N = 4, 6, 7

        s_const = sem("s_const")
        s_stage = sem("s_stage")
        s_wd_in = sem("s_wd_in")
        s_wsplit = sem("s_wsplit")
        x_loaded = [sem(f"x_loaded{q}") for q in range(4)]
        y_stored = [sem(f"y_stored{q}") for q in range(4)]
        s_xagg = sem("s_xagg")
        s_gavg = sem("s_gavg")
        s_gsq = sem("s_gsq")
        s_vchain = sem("s_vchain")
        s_carry_a = sem("s_carry_a")
        s_gh = sem("s_gh")
        s_gl = sem("s_gl")
        s_chunk_used = sem("s_chunk_used")
        s_gram = sem("s_gram")
        s_masked = sem("s_masked")
        s_turned = sem("s_turned")
        s_after = sem("s_after")
        s_pick = sem("s_pick")
        s_sq = sem("s_sq")
        s_norm = sem("s_norm")
        s_root = sem("s_root")
        s_rinv = sem("s_rinv")
        s_fn = sem("s_fn")
        s_th = sem("s_th")
        s_t = sem("s_t")
        s_conv = sem("s_conv")
        s_relu = sem("s_relu")
        s_added = sem("s_added")
        s_y = sem("s_y")
        s_ymv = sem("s_ymv")
        s_yagg = sem("s_yagg")
        s_newton = sem("s_newton")
        s_issue = sem("s_issue")
        s_carry = sem("s_carry")
        s_w12 = sem("s_w12")
        s_link = sem("s_link")
        s_sstat = sem("s_sstat")
        s_smm = sem("s_smm")
        s_sroot = sem("s_sroot")
        s_iota = sem("s_iota")
        s_sorted = sem("s_sorted")
        s_recs = sem("s_recs")
        s_rec = sem("s_rec")
        s_onehot = sem("s_onehot")
        s_at = sem("s_at")
        s_placed = sem("s_placed")
        s_pads = sem("s_pads")
        s_idx = sem("s_idx")
        gathered = [sem(f"gathered{b}") for b in range(BUFS)]
        written = [sem(f"written{b}") for b in range(BUFS)]
        s_ypad = sem("s_ypad")
        s_rows = sem("s_rows")
        s_own = sem("s_own")
        s_pool = sem("s_pool")
        s_diag = sem("s_diag")
        s_mix = sem("s_mix")
        s_res = sem("s_res")

        block = ctx.enter_context(nc.Block())

        STATS_CHAIN = 7
        STATS_AT = 4

        def xs(ct, lo, n, par):
            return arena[:, bass.ds(par * (CT * PIX) + (ct * PIX + lo), n)]

        def gram_parts(t):
            parts, row = [], 2 * t
            while row < min(2 * t + 4, H):
                end = min(2 * t + 4, H, (row // (RING * ROWS) + 1) * RING * ROWS)
                parts.append(((row - 2 * t) * W, (row % (RING * ROWS)) * W, (end - row) * W))
                row = end
            return parts

        @block.sync
        def _(sp):
            sp.dma_start(cst[:, :], consts[:, :]).then_inc(s_const, 16)
            sp.dma_start(bias_sb[:, :], bias.rearrange("(t p) -> p t", p=P),
                         allow_slow_non_contiguous=True).then_inc(s_const, 16)
            for q in range(4):
                sp.dma_start(xs_quarter(0, q), x_v[0, :, :, q * 1024:(q + 1) * 1024]).then_inc(x_loaded[q], 16)
                if q == 0:
                    sp.dma_start(stage_w, wt[0:C, :].rearrange("(t p) n -> p t n", p=P)).then_inc(s_const, 16)
                if q == 1:
                    sp.wait_ge(s_stage, 1)
                    for rep in range(3):
                        sp.dma_start(stage_d[32 * rep:32 * rep + D, :], wturn[:, :]).then_inc(s_wd_in, 16)

            sp.wait_ge(s_wsplit, 6)
            sp.wait_ge(s_vchain, 1)
            for q in range(4):
                sp.dma_start(xs_quarter(1, q), x_v[1, :, :, q * 1024:(q + 1) * 1024]).then_inc(x_loaded[q], 16)

            def quarters(i, load_next):
                for q in range(4):
                    sp.wait_ge(s_y, i * (CH * CT) + (q + 1) * 2 * CT)
                    sp.dma_start(y_v[bass.ds(i, 1), :, :, q * 1024:(q + 1) * 1024].rearrange("b p t n -> p (b t) n"),
                                 xs_quarter(i % 2, q)).then_inc(y_stored[q], 16)
                    if load_next and q > 0:
                        load(i, q - 1)
                if load_next:
                    load(i, 3)

            def load(i, q):
                sp.wait_ge(y_stored[q], (i + 1) * 16)
                sp.dma_start(xs_quarter(i % 2, q),
                             x_v[bass.ds(i + 2, 1), :, :, q * 1024:(q + 1) * 1024].rearrange("b p t n -> p (b t) n"))\
                  .then_inc(x_loaded[q], 16)

            if B > 2:
                with sp.Fori(0, B - 2) as i:
                    quarters(i, True)
            quarters(B - 2, False)
            for q in range(4):
                sp.wait_ge(y_stored[q], 16 * (B - 1))
            sp.dma_start(w1_sb, w1t.rearrange("(t p) e -> p t e", p=P)).then_inc(s_w12, 16)
            sp.dma_start(w2_sb[0:HID, :], w2t[:, :]).then_inc(s_w12, 16)
            sp.dma_start(b1_sb[0:HID, :], b1.rearrange("(e a) -> e a", a=1)).then_inc(s_w12, 16)
            sp.dma_start(b2_sb, b2.rearrange("(t p) -> p t", p=P), allow_slow_non_contiguous=True).then_inc(s_w12, 16)
            quarters(B - 1, False)
            sp.wait_ge(s_recs, 1)
            sp.dma_start(rec_dram.rearrange("(n p) e -> p n e", p=P), recs).then_inc(s_rec, 16)
            for q in range(4):
                sp.wait_ge(y_stored[q], 16 * B)

        @block.gpsimd
        def _(pool):
            pool.memset(stage_d, 0.0).then_inc(s_stage, 1)

            def image(i):
                for c in range(CH):
                    n = i * CH + c
                    th = tpair[0:REP, c % 2, :]
                    pool.wait_ge(s_fn, n + 1)
                    if not (isinstance(i, int) and i == 0 and c < 2):
                        pool.wait_ge(s_conv, (i * CH + c - 1) * CT)
                    pool.sem_inc(s_issue, 1)
                    pool.tensor_copy(th, fn[0:REP, :]).then_inc(s_th, 1)
                    pool.wait_ge(s_th, n + 1)
                    tl = tpair[64:96, c % 2, :]
                    pool.tensor_tensor(tl, fn[64:96, :], tl, ALU.subtract).then_inc(s_t, 1)

            image(0)
            with pool.Fori(1, B) as i:
                image(i)

            pool.wait_ge(s_conv, B * CH * CT)
            pool.iota(plane_i.rearrange("p (n a) -> p n a", a=1), [[C, B], [P, CT]], base=0, channel_multiplier=1)\
                .then_inc(s_iota, 1)
            pool.iota(tnum_i, [[1, NT]], base=0, channel_multiplier=0).then_inc(s_iota, 1)
            pool.iota(lane_i, [[1, P]], base=0, channel_multiplier=0).then_inc(s_iota, 1)
            pool.wait_ge(s_sorted, 1)
            for q in range(4):
                pool.wait_ge(y_stored[q], 16 * B)
            pool.wait_ge(s_rec, 16)

            def class_of(t):
                return pool.value_load(cls_i[0:1, bass.ds(t, 1)], min_val=0, max_val=NCLS)

            def gather(t, b):
                pool.sem_inc(s_issue, 1)
                pool.memset(recs_in[:, b, :], 0.0)
                pool.tensor_copy(idx[:, b:b + 1], ids_i[:, bass.ds(t, 1)]).then_inc(s_idx, 1)
                pool.wait_ge(s_idx, t + 1)
                pool.sem_inc(s_issue, 1)
                with pool.If(class_of(t) < NCLS):
                    pool.indirect_dma_start(out=recs_in[:, b, :], out_offset=None, in_=rec_dram[:, :],
                                            in_offset=bass.IndirectOffsetOnAxis(ap=idx[:, b:b + 1], axis=0),
                                            bounds_check=NPL - 1, oob_is_err=False).then_inc(gathered[b], 16)
                    pool.indirect_dma_start(out=bufs[:, b, :], out_offset=None, in_=y_dram[:, :],
                                            in_offset=bass.IndirectOffsetOnAxis(ap=idx[:, b:b + 1], axis=0),
                                            bounds_check=NPL - 1, oob_is_err=False).then_inc(gathered[b], 16)
                with pool.Else():
                    pool.dma_start(bufs[0:1, b, 0:REC], rec_dram[0:1, :]).then_inc(gathered[b], 16)
                    pool.dma_start(recs_in[0:1, b, :], rec_dram[0:1, :]).then_inc(gathered[b], 16)

            def scatter(t, b):
                pool.wait_ge(s_res, (t + 1) * 8)
                pool.sem_inc(s_issue, 1)
                with pool.If(class_of(t) < NCLS):
                    pool.indirect_dma_start(out=out_rows[:, :],
                                            out_offset=bass.IndirectOffsetOnAxis(ap=idx[:, b:b + 1], axis=0),
                                            in_=bufs[:, b, :], in_offset=None,
                                            bounds_check=NPL - 1, oob_is_err=False).then_inc(written[b], 16)
                with pool.Else():
                    pool.dma_start(no_out[bass.ds(t, 1), :], bufs[0:1, b, 0:REC]).then_inc(written[b], 16)

            def step(t, u):
                if not (isinstance(t, int) and t < 2):
                    pool.wait_ge(written[(u + 2) % BUFS], ((t - 2) // BUFS + 1) * 16 if isinstance(t, int)
                                 else turn_of(t, u - 2))
                if not (isinstance(t, int) and t + 2 >= NT):
                    gather(t + 2, (u + 2) % BUFS)
                if not (isinstance(t, int) and t < 1):
                    scatter(t - 1, (u - 1) % BUFS)

            gather(0, 0)
            gather(1, 1)
            for u in range(BUFS):
                step(u, u)
            with pool.Fori(1, NT // BUFS - 1) as g:
                def turn_of(t, back):
                    return (g + (1 if back >= 0 else 0)) * 16
                for u in range(BUFS):
                    step(g * BUFS + u, u)
            for u in range(BUFS):
                step(NT - BUFS + u, u)
            scatter(NT - 1, BUFS - 1)
            for b in range(BUFS):
                pool.wait_ge(written[b], NT // BUFS * 16)

        @block.scalar
        def _(act):
            def group_root(k):
                act.wait_ge(s_gavg, 2 * k + 2)
                act.activation(grs[:, :], psum[:, BANK_N, CT:2 * CT], ACT.Sqrt, bias=epsg[:, :]).then_inc(s_gsq, 1)

            def normalise(i, c, first=False):
                n0 = (i * CH + c) * CT
                act.wait_ge(s_newton, 3 * i + 3)
                if not first:
                    act.wait_ge(s_chunk_used, i * CH + c - RING + 1)
                for ct in range(CT):
                    if not (isinstance(n0, int) and n0 + ct < 2):
                        act.wait_ge(s_gl, n0 + ct - 1)
                    act.sem_inc(s_carry_a, 1)
                    piece = xs(ct, c * CW, CW, i % 2)
                    act.activation(g32[:, ct % 2, :], piece, ACT.Identity, bias=gbias[:, ct:ct + 1],
                                   scale=grstd[:, ct:ct + 1])
                    act.activation(gh[:, ct, (c % RING) * CW:(c % RING + 1) * CW], piece, ACT.Identity,
                                   bias=gbias[:, ct:ct + 1], scale=grstd[:, ct:ct + 1]).then_inc(s_gh, 1)

            def conv_out(chunk, o):
                n = chunk * CT + o
                act.wait_ge(s_conv, n + 1)
                if isinstance(n, int) and n < 2:
                    pass
                else:
                    act.wait_ge(s_added, n - 1)
                act.activation(relu[:, o % 2, :], psum[:, o, :], ACT.Relu, bias=bias_sb[:, o:o + 1],
                               scale=1.0 / (SC * SC)).then_inc(s_relu, 1)

            def after(i, c):
                act.wait_ge(s_turned, i * CH + c + 1)
                half = (c % 2) * PAIRS * P
                n = (PAIRS - 1) * P if c == CH - 1 else PAIRS * P
                act.activation(bq[:, AFTER, half:half + n], psum[:, BANK_N, 0:n], ACT.Copy).then_inc(s_after, 1)

            def image(i, last):
                for c in range(CH):
                    n = i * CH + c
                    first = isinstance(n, int) and n == 0
                    act.wait_ge(s_pick, n + 1)
                    act.activation(sq[0:D, :], psum[0:D, BANK_A, :], ACT.Square).then_inc(s_sq, 1)
                    if not first:
                        conv_out(n - 1, 0)
                        conv_out(n - 1, 1)
                    act.wait_ge(s_norm, n + 1)
                    act.activation(sq[0:REP, :], psum[0:REP, BANK_N, :], ACT.Sqrt,
                                   bias=epsd[0:REP, :]).then_inc(s_root, 1)
                    if not first:
                        conv_out(n - 1, 2)
                        conv_out(n - 1, 3)
                    if c + 1 < CH:
                        after(i, c + 1)
                    elif not last:
                        after(i + 1, 0)
                    if c + 3 < CH:
                        normalise(i, c + 3, first=first)
                    elif not last:
                        normalise(i + 1, c + 3 - CH)
                    if c == STATS_AT and not last:
                        group_root(i + 1)

            act.wait_ge(s_wsplit, 1)
            group_root(0)
            for c in range(3):
                normalise(0, c, first=True)
            after(0, 0)
            image(0, False)
            if B > 2:
                with act.Fori(1, B - 1) as i:
                    image(i, False)
            image(B - 1, True)
            for o in range(CT):
                conv_out(B * CH - 1, o)

            act.wait_ge(s_smm, 2)
            act.activation(sr, psum[:, 1, 0:NC], ACT.Sqrt, bias=epsg[:, :]).then_inc(s_sroot, 1)

            def pad_plane(t, u):
                act.wait_ge(gathered[u], turns_done(t, u))
                if not (isinstance(t, int) and t == 0):
                    act.wait_ge(s_rows, t)
                with act.If(class_of(t) < NCLS):
                    act.activation(ypad[:, :, PADC:PADC + W], bufs[:, u, :].rearrange("p (h w) -> p h w", w=W),
                                   ACT.Copy).then_inc(s_ypad, 1)
                with act.Else():
                    if not (isinstance(t, int) and t == 0):
                        act.wait_ge(s_ypad, t)
                    act.sem_inc(s_ypad, 1)

            def diagonals(t, u):
                s = u % 2
                if not (isinstance(t, int) and t < 2):
                    act.wait_ge(s_res, (t - 1) * 8)
                for k in range(3):
                    act.activation(diag[:, s, k, :], ident, ACT.Copy, scale=recs_in[:, u, k:k + 1])
                act.activation(const_t[:, s:s + 1], recs_in[:, u, 3:4], ACT.Copy).then_inc(s_diag, 1)

            def results(t, u):
                act.wait_ge(s_diag, t + 1)
                with act.If(class_of(t) < NCLS):
                    for b in range(8):
                        act.wait_ge(s_mix, t * 8 + b + 1)
                        act.activation(bufs[:, u, b * CW:(b + 1) * CW], psum[:, b, :], ACT.Identity,
                                       bias=const_t[:, u % 2:u % 2 + 1]).then_inc(s_res, 1)
                with act.Else():
                    act.wait_ge(s_mix, t * 8 + 8)
                    if not (isinstance(t, int) and t == 0):
                        act.wait_ge(s_res, t * 8)
                    act.sem_inc(s_res, 8)

            def class_of(t):
                return act.value_load(cls_i[0:1, bass.ds(t, 1)], min_val=0, max_val=NCLS)

            def turns_done(t, u):
                return (t // BUFS + 1) * 32 if isinstance(t, int) else turns[0](t, u)

            turns = [None]

            def step(t, u):
                if not (isinstance(t, int) and t + 1 >= NT):
                    pad_plane(t + 1, (u + 1) % BUFS)
                if not (isinstance(t, int) and t == 0):
                    results(t - 1, (u - 1) % BUFS)
                if not (isinstance(t, int) and t + 1 >= NT):
                    diagonals(t + 1, (u + 1) % BUFS)

            act.wait_ge(s_pads, 2)
            act.wait_ge(s_sorted, 1)
            pad_plane(0, 0)
            diagonals(0, 0)
            for u in range(BUFS):
                step(u, u)
            with act.Fori(1, NT // BUFS - 1) as g:
                turns[0] = lambda t, u: (g + (2 if u == 0 else 1)) * 32
                for u in range(BUFS):
                    step(g * BUFS + u, u)
            for u in range(BUFS):
                step(NT - BUFS + u, u)
            results(NT - 1, BUFS - 1)

        @block.vector
        def _(dve):
            def split_conv_weights():
                dve.wait_ge(s_const, 48)
                dve.tensor_scalar(stage_w, stage_w, SC, None, ALU.mult).then_inc(s_wsplit, 1)
                dve.wait_ge(s_wsplit, 1)
                dve.tensor_copy(wh, stage_w).then_inc(s_wsplit, 1)
                dve.wait_ge(s_wsplit, 2)
                dve.tensor_tensor(wl, stage_w, wh, ALU.subtract).then_inc(s_wsplit, 1)

            def split_descriptor_weights():
                dve.wait_ge(s_wd_in, 48)
                dve.tensor_scalar(stage_d, stage_d, SC, None, ALU.mult).then_inc(s_wsplit, 1)
                dve.wait_ge(s_wsplit, 4)
                dve.tensor_copy(wd, stage_d).then_inc(s_wsplit, 1)
                dve.wait_ge(s_wsplit, 5)
                dve.tensor_tensor(wd[32:64, :], stage_d[32:64, :], wd[32:64, :], ALU.subtract).then_inc(s_wsplit, 1)

            def x_stats(i, q, ct):
                if ct == 0:
                    dve.wait_ge(x_loaded[q], (i + 1) * 16)
                for c in (2 * q, 2 * q + 1):
                    last = dve.bn_stats(bnx[:, ct, c, :], xs(ct, c * CW, CW, i % 2))
                if q == 3 and ct == CT - 1:
                    last.then_inc(s_vchain, 1)

            def group_sums(i):
                b = i * STATS_CHAIN
                dve.wait_ge(s_vchain, b + 1)
                dve.sem_inc(s_carry, 1)
                for ct in range(CT):
                    last = dve.bn_aggr(aggx[:, ct, :], bnx[:, ct, :, :].rearrange("p c s -> p (c s)"))
                last.then_inc(s_xagg, 1)

            def group_spreads(i):
                b = i * STATS_CHAIN
                dve.wait_ge(s_xagg, 2 * i + 1)
                dve.wait_ge(s_gavg, 2 * i + 1)
                dve.tensor_copy(gm[:, :], psum[:, BANK_N, 0:CT]).then_inc(s_vchain, 1)
                dve.wait_ge(s_vchain, b + 2)
                dve.tensor_tensor(gd[:, :], aggx[:, :, 0], gm[:, :], ALU.subtract).then_inc(s_vchain, 1)
                dve.wait_ge(s_vchain, b + 3)
                dve.tensor_tensor(gd[:, :], gd[:, :], gd[:, :], ALU.mult).then_inc(s_vchain, 1)
                dve.wait_ge(s_vchain, b + 4)
                dve.tensor_tensor(gd[:, :], gd[:, :], aggx[:, :, 1], ALU.add).then_inc(s_xagg, 1)

            def group_values(i):
                b = i * STATS_CHAIN
                dve.wait_ge(s_gsq, i + 1)
                dve.reciprocal(gd[:, :], grs[:, :]).then_inc(s_vchain, 1)
                dve.wait_ge(s_vchain, b + 5)
                dve.tensor_tensor(grs[:, :], gd[:, :], gd[:, :], ALU.mult).then_inc(s_vchain, 1)
                dve.wait_ge(s_vchain, b + 6)
                dve.scalar_tensor_tensor(grs[:, :], psum[:, BANK_N, CT:2 * CT], EPS, grs[:, :],
                                         ALU.add, ALU.mult).then_inc(s_vchain, 1)
                dve.wait_ge(s_vchain, b + 7)
                dve.tensor_scalar(grs[:, :], grs[:, :], -0.5 * SC, 1.5 * SC, ALU.mult, ALU.add).then_inc(s_newton, 1)
                dve.wait_ge(s_newton, 3 * i + 1)
                dve.tensor_tensor(grstd[:, :], grs[:, :], gd[:, :], ALU.mult).then_inc(s_newton, 1)
                dve.wait_ge(s_newton, 3 * i + 2)
                dve.scalar_tensor_tensor(gbias[:, :], gm[:, :], -1.0, grstd[:, :], ALU.mult, ALU.mult)\
                    .then_inc(s_newton, 1)

            def low_parts(i, c, stats=None):
                n0 = (i * CH + c) * CT
                slot = slice((c % RING) * CW, (c % RING + 1) * CW)
                for ct in range(CT):
                    dve.wait_ge(s_gh, n0 + ct + 1)
                    dve.tensor_tensor(gl[:, ct, slot], g32[:, ct % 2, :], gh[:, ct, slot],
                                      ALU.subtract).then_inc(s_gl, 1)
                    if stats:
                        stats(ct)

            def mask(i, t):
                dve.wait_ge(s_gram, i * NB + t + 1)
                bank = GRAM0 + t % 2
                same, before_ = (t % PRING) * P, ((t + 1) % PRING) * P
                if t + 1 < NB and before_:
                    base = bq_off + SAME * PRING * P + same
                    dst = arena[:, base:base + 2 * (PRING + 1) * P]\
                        .rearrange("p (r n) -> p r n", r=2)[:, :, 0:P]
                    dve.tensor_tensor(dst, psum[:, bank, 0:2 * P].rearrange("p (r n) -> p r n", r=2),
                                      band.unsqueeze(1).to_broadcast([P, 2, P]), ALU.mult).then_inc(s_masked, 1)
                    return
                if t + 1 < NB:
                    dve.tensor_tensor(bq[:, BEFORE, before_:before_ + P], psum[:, bank, P:2 * P], band, ALU.mult)
                dve.tensor_tensor(bq[:, SAME, same:same + P], psum[:, bank, 0:P], band, ALU.mult).then_inc(s_masked, 1)

            def residual(i, c, o):
                n = (i * CH + c) * CT + o
                y = xs(o, c * CW, CW, i % 2)
                dve.wait_ge(s_relu, n + 1)
                dve.tensor_tensor(y, y, relu[:, o % 2, :], ALU.add).then_inc(s_added, 1)
                dve.wait_ge(s_added, n + 1)
                dve.bn_stats(bny[:, o, c, :], y).then_inc(s_y, 1)

            def descriptor(i, c):
                n = i * CH + c
                dve.wait_ge(s_root, n + 1)
                dve.reciprocal(sq[0:REP, :], sq[0:REP, :]).then_inc(s_rinv, 1)
                dve.wait_ge(s_rinv, n + 1)
                if not (isinstance(n, int) and n == 0):
                    dve.wait_ge(s_t, n)
                dve.tensor_tensor(fn[0:REP, :], psum[0:REP, BANK_A, :], sq[0:REP, :], ALU.mult).then_inc(s_fn, 1)

            def masks_of(i, c, between):
                if not (isinstance(i, int) and i == 0 and c == 0):
                    dve.wait_ge(s_pick, i * CH + c)
                for k in range(PAIRS):
                    mask(i, PAIRS * c + k)
                    if between:
                        between[k]()

            def image(i, first, last):
                for c in range(CH):
                    if c > 0:
                        res = [lambda o=o: residual(i, c - 1, o) for o in range(CT)]
                    elif first:
                        res = []
                    else:
                        res = [lambda o=o: residual(i - 1, CH - 1, o) for o in range(CT)]
                    if c + 1 < CH:
                        masks_of(i, c + 1, res)
                    elif not last:
                        masks_of(i + 1, 0, res)
                    else:
                        for f in res:
                            f()
                    descriptor(i, c)
                    if c == STATS_AT and not last:
                        group_spreads(i + 1)
                    if c == 0 and not first:
                        keep_stats(i - 1)
                    if c + 3 < CH:
                        low_parts(i, c + 3, (lambda ct: x_stats(i + 1, c, ct)) if c < 4 and not last else None)
                    elif not last:
                        low_parts(i + 1, c + 3 - CH)
                    if c == STATS_AT - 1 and not last:
                        group_sums(i + 1)
                    if c == STATS_AT and not last:
                        group_values(i + 1)

            def keep_stats(i):
                dve.wait_ge(s_y, (i + 1) * CH * CT)
                dve.sem_inc(s_carry, 1)
                for ct in range(CT):
                    ins = dve.bn_aggr(aggy[:, ct, :], bny[:, ct, :, :].rearrange("p c s -> p (c s)"))
                ins.then_inc(s_yagg, 1)
                dve.wait_ge(s_yagg, i + 1)
                dve.tensor_copy(ymv[:, bass.ds(i * (2 * CT), 2 * CT)],
                                aggy[:, :, :].rearrange("p t s -> p (t s)")).then_inc(s_ymv, 1)

            def sort_planes():
                links = [0]

                def link(ins):
                    links[0] += 1
                    ins.then_inc(s_link, 1)
                    dve.wait_ge(s_link, links[0])

                stats = ymv[:, :].rearrange("p (n s) -> p n s", s=2)
                dve.wait_ge(s_ymv, B)
                dve.wait_ge(s_conv, B * CH * CT)
                dve.memset(zeros, 0.0)
                dve.tensor_copy(sm, stats[:, :, 0]).then_inc(s_sstat, 1)
                dve.wait_ge(s_smm, 1)
                link(dve.tensor_tensor(sd, sm, psum[:, 0, 0:NC], ALU.subtract))
                link(dve.tensor_tensor(tmp, sd, sd, ALU.mult))
                dve.tensor_tensor(tmp, tmp, stats[:, :, 1], ALU.add).then_inc(s_sstat, 1)
                dve.wait_ge(s_sroot, 1)
                link(dve.reciprocal(sa, sr))
                link(dve.tensor_tensor(sr, sa, sa, ALU.mult))
                link(dve.scalar_tensor_tensor(sr, psum[:, 1, 0:NC], EPS, sr, ALU.add, ALU.mult))
                link(dve.tensor_scalar(sr, sr, -0.5, 1.5, ALU.mult, ALU.add))
                link(dve.tensor_tensor(sa, sr, sa, ALU.mult))
                link(dve.scalar_tensor_tensor(scc, psum[:, 0, 0:NC], -1.0, sa, ALU.mult, ALU.mult))
                dve.tensor_tensor(sgap, sd, sa, ALU.mult).then_inc(s_sstat, 1)
                dve.wait_ge(s_w12, 64)
                dve.wait_ge(s_smm, 3)
                dve.tensor_scalar(hid[0:HID, :], psum[0:HID, 2, 0:B], b1_sb[0:HID, :], 0.0, ALU.add, ALU.max)\
                    .then_inc(s_sstat, 1)
                dve.wait_ge(s_smm, 4)
                link(dve.tensor_tensor(score.rearrange("p (b t) -> p b t", t=CT),
                                       psum[:, 3, 0:NC].rearrange("p (t b) -> p b t", t=CT),
                                       b2_sb.unsqueeze(1).to_broadcast([P, B, CT]), ALU.add))
                link(dve.tensor_scalar(score, score, 0.0, None, ALU.max))
                link(dve.tensor_scalar(cls, score, 1.0, None, ALU.is_ge))
                for k in range(2, NCLS):
                    link(dve.scalar_tensor_tensor(cls, score, float(k), cls, ALU.is_ge, ALU.add))
                for k in range(NCLS):
                    ins = dve.tensor_scalar(onehot[:, k * NC:(k + 1) * NC], cls, float(k), None, ALU.is_equal)
                ins.then_inc(s_sstat, 1)
                link(dve.scalar_tensor_tensor(fs, cls, 1.0, score, ALU.add, ALU.subtract))
                link(dve.tensor_tensor(fb, score, cls, ALU.subtract))
                dve.wait_ge(s_iota, 3)
                dve.tensor_copy(lane, lane_i)
                dve.tensor_copy(tnum, tnum_i)
                link(dve.tensor_copy(plane_f, plane_i))
                dve.tensor_scalar(plane_f, plane_f, 1.0, None, ALU.add)
                link(dve.tensor_tensor(recs[:, :, 1], fs, sa, ALU.mult))
                dve.tensor_tensor(recs[:, :, 2], fb, sa, ALU.mult)
                link(dve.tensor_tensor(tmp, onehot[:, 0:NC], recs[:, :, 1], ALU.mult))
                link(dve.scalar_tensor_tensor(recs[:, :, 0], sa, 1.0, tmp, ALU.add, ALU.add))
                link(dve.scalar_tensor_tensor(tmp, fs, 1.0, fb, ALU.add, ALU.add))
                dve.tensor_tensor(recs[:, :, 3], tmp, scc, ALU.mult).then_inc(s_recs, 1)
                dve.wait_ge(s_smm, 6)
                for k in range(NCLS):
                    cols = slice(k * NC, (k + 1) * NC)
                    ins = dve.tensor_tensor_scan(incl[:, cols], psum[:, 5, cols], zeros, 0.0, ALU.add, ALU.add)
                link(ins)
                link(dve.tensor_tensor(rank, incl, psum[:, 5, 0:NCLS * NC], ALU.subtract))
                link(dve.tensor_tensor(rank, rank, psum[:, 4, 0:NCLS * NC], ALU.add))
                totals = incl.rearrange("p (k n) -> p k n", k=NCLS)[:, :, NC - 1]
                link(dve.tensor_scalar(tiles, totals, 1.0 / P, 0.5 - 0.5 / P, ALU.mult, ALU.add))
                link(dve.tensor_scalar(tiles, tiles, MAGIC, None, ALU.add))
                link(dve.tensor_scalar(tiles, tiles, -MAGIC, None, ALU.add))
                link(dve.tensor_tensor_scan(tincl, tiles, zeros[:, 0:NCLS], 0.0, ALU.add, ALU.add))
                link(dve.tensor_tensor(tbase, tincl, tiles, ALU.subtract))
                link(dve.tensor_scalar(tb128, tbase, float(P), None, ALU.mult))
                for k in range(NCLS):
                    cols = slice(k * NC, (k + 1) * NC)
                    ins = dve.scalar_tensor_tensor(rank[:, cols], rank[:, cols], tb128[:, k:k + 1], onehot[:, cols],
                                                   ALU.add, ALU.mult)
                link(ins)
                link(dve.tensor_reduce(slot, rank.rearrange("p (k n) -> p n k", k=NCLS), AX.X, ALU.add))
                link(dve.tensor_scalar(slot_hi, slot, 1.0 / P, 0.5 / P - 0.5, ALU.mult, ALU.add))
                link(dve.tensor_scalar(slot_hi, slot_hi, MAGIC, None, ALU.add))
                link(dve.tensor_scalar(slot_hi, slot_hi, -MAGIC, None, ALU.add))
                link(dve.scalar_tensor_tensor(slot_lo, slot_hi, -float(P), slot, ALU.mult, ALU.add))

                def place(g, u):
                    if not (isinstance(g, int) and g < 2):
                        dve.wait_ge(s_placed, g - 1)
                        dve.sem_inc(s_carry, 1)
                    cols = bass.ds(g * COLS, COLS)
                    dve.tensor_tensor(at_lane[:, u, :, :], lane.unsqueeze(1).to_broadcast([P, COLS, P]),
                                      slot_lo[:, cols].unsqueeze(2).to_broadcast([P, COLS, P]), ALU.is_equal)
                    dve.tensor_tensor(at_tile[:, u, :, :], tnum.unsqueeze(1).to_broadcast([P, COLS, NT]),
                                      slot_hi[:, cols].unsqueeze(2).to_broadcast([P, COLS, NT]), ALU.is_equal)\
                        .then_inc(s_onehot, 1)
                    dve.wait_ge(s_onehot, g + 1)
                    dve.sem_inc(s_carry, 1)
                    dve.tensor_tensor(at_tile[:, u, :, :], at_tile[:, u, :, :],
                                      plane_f[:, cols].unsqueeze(2).to_broadcast([P, COLS, NT]), ALU.mult)\
                        .then_inc(s_at, 1)

                place(0, 0)
                place(1, 1)
                if NC // COLS > 2:
                    with dve.Fori(1, NC // (2 * COLS)) as h:
                        for u in range(2):
                            place(h * 2 + u, u)
                link(dve.tensor_scalar(tcls, tnum, tincl[:, 0:1], None, ALU.is_ge))
                for k in range(1, NCLS):
                    link(dve.scalar_tensor_tensor(tcls, tnum, tincl[:, k:k + 1], tcls, ALU.is_ge, ALU.add))
                dve.tensor_copy(cls_i, tcls)
                dve.wait_ge(s_placed, NC // COLS)
                link(dve.tensor_scalar(empty, psum[:, 6, 0:NT], 0.0, NPL + 1.0, ALU.is_equal, ALU.mult))
                link(dve.scalar_tensor_tensor(ids, psum[:, 6, 0:NT], -1.0, empty, ALU.add, ALU.add))
                dve.tensor_copy(ids_i, ids).then_inc(s_sorted, 1)

            OWN = 22

            def pools(t, s, k):
                used = [0]

                def op(dst, a, b, wait=True, signal=s_own):
                    if wait and used[0]:
                        dve.wait_ge(s_own, t * OWN + used[0])
                    ins = dve.tensor_tensor(dst, a, b, ALU.max)
                    ins.then_inc(signal, 1)
                    if signal is s_own:
                        used[0] += 1

                def window(src, mid, dst, r, signal=s_own):
                    m, w = half_m, half_w
                    op(mid(m, 0, 31 + r), src(1 - r, 31 + r), src(2 - r, 31 + r))
                    core = m
                    if r in (2, 4):
                        op(mid(w, 0, 30 + r), mid(m, 0, 30 + r), mid(m, 1, 30 + r))
                        core = w
                    if r == 4:
                        op(mid(m, 0, 32), mid(w, 0, 32), mid(w, 2, 32))
                        core = m
                    if r in (3, 5):
                        op(mid(w, 0, 14 + (r + 1) // 2, 1), mid(m, 1, 14 + (r + 1) // 2, 2),
                           mid(m, 2, 14 + (r + 1) // 2, 2))
                        if r == 5:
                            op(mid(w, 0, 16, 1), mid(w, 0, 16, 1), mid(w, 1, 16, 1))
                        op(mid(m, 0, 16, 2), mid(w, 0, 16, 1), mid(m, 0, 16, 2))
                        op(mid(m, 1, 16, 2), mid(w, 0, 16, 1), mid(m, r, 16, 2), wait=False)
                    op(dst(0), mid(core, 0, 32), src(-r, 32))
                    op(dst(1), mid(core, 0, 32), src(1 + r, 32), wait=False, signal=signal)

                def cols(i, n):
                    return ypad[:, :, PADC + i:PADC + i + 2 * n - 1:2]

                def cols_mid(a, i, n, step=1):
                    return a.rearrange("p (h w) -> p h w", w=36)[:, :, i:i + step * (n - 1) + 1:step]

                def rows(i, n):
                    return hbuf[:, PADC + i:PADC + i + 2 * n - 1:2, :]

                def rows_mid(a, i, n, step=1):
                    return a.rearrange("p (h w) -> p h w", w=W)[:, i:i + step * (n - 1) + 1:step, :]

                sm_, bg = small[:, s, :, :], big[:, s, :].rearrange("p (h w) -> p h w", w=W)
                inner = hbuf[:, PADC:PADC + H, :]
                window(cols, cols_mid, lambda e: inner[:, :, e::2], max(k, 1), signal=s_rows)
                dve.wait_ge(s_rows, t + 1)
                if k == 0:
                    window(rows, rows_mid, lambda e: bg[:, e::2, :], 1, signal=s_pool)
                else:
                    window(rows, rows_mid, lambda e: sm_[:, e::2, 1:W + 1], k)
                    op(inner, sm_[:, :, 0:W], sm_[:, :, 2:W + 2])
                    op(bg, hbuf[:, PADC - 1:PADC - 1 + H, :], hbuf[:, PADC + 1:PADC + 1 + H, :], signal=s_pool)
                assert used[0] <= OWN
                dve.sem_inc(s_own, OWN - used[0])

            def tile(t, s):
                cls_t = dve.value_load(cls_i[0:1, bass.ds(t, 1)], min_val=0, max_val=NCLS)

                def waits():
                    dve.wait_ge(s_ypad, t + 1)
                    if not (isinstance(t, int) and t < 2):
                        dve.wait_ge(s_mix, (t - 1) * 8)
                    if not (isinstance(t, int) and t == 0):
                        dve.wait_ge(s_pool, t)

                def branch(lo, hi):
                    if lo == hi:
                        waits()
                        if lo == NCLS:
                            dve.sem_inc(s_own, OWN)
                            dve.sem_inc(s_rows, 1)
                            dve.sem_inc(s_pool, 1)
                        else:
                            pools(t, s, lo)
                        return
                    mid = (lo + hi) // 2
                    with dve.If(cls_t < mid + 1):
                        branch(lo, mid)
                    with dve.Else():
                        branch(mid + 1, hi)

                branch(0, NCLS)

            dve.memset(epsd[:, :], EPS_D * SC * SC)
            dve.memset(epsg[:, :], EPS)
            for q in range(4):
                for ct in range(CT):
                    x_stats(0, q, ct)
                if q == 0:
                    split_conv_weights()
                if q == 1:
                    split_descriptor_weights()
            group_sums(0)
            group_spreads(0)
            group_values(0)
            for c in range(3):
                low_parts(0, c)
            masks_of(0, 0, [])
            image(0, True, False)
            if B > 2:
                with dve.Fori(1, B - 1) as i:
                    image(i, False, False)
            image(B - 1, False, True)
            for o in range(CT):
                residual(B - 1, CH - 1, o)
            keep_stats(B - 1)
            sort_planes()
            for q in range(4):
                dve.wait_ge(y_stored[q], 16 * B)
            for side in (slice(0, PADC), slice(PADC + W, WP)):
                dve.memset(ypad[:, :, side], LOWEST)
            for side in (slice(0, PADC), slice(PADC + H, H + 2 * PADC)):
                dve.memset(hbuf[:, side, :], LOWEST)
            dve.wait_ge(s_rec, 16)
            for s in range(2):
                dve.memset(small[:, s, :, 0:W + 2:W + 1], LOWEST).then_inc(s_pads, 1)
            dve.wait_ge(s_pads, 2)
            for t in range(2):
                tile(t, t)
            with dve.Fori(1, NT // 2) as g:
                for s in range(2):
                    tile(g * 2 + s, s)

        @block.tensor
        def _(pe):
            def product(dst, w, m, k, nk):
                return pe.matmul(dst, w, m, start=(k == 0), stop=(k == nk - 1))

            def gram(i, t):
                if not (isinstance(i, int) and i == 0 and t < 2):
                    pe.wait_ge(s_masked, i * NB + t - 1)
                own = ((2 * t) % (RING * ROWS)) * W
                for col, ring, n in gram_parts(t):
                    for ct in range(CT):
                        sh, sl = gh[:, ct, own:own + 2 * W], gl[:, ct, own:own + 2 * W]
                        mh, ml = gh[:, ct, ring:ring + n], gl[:, ct, ring:ring + n]
                        dst = psum[:, GRAM0 + t % 2, col:col + n]
                        product(dst, sh, mh, 3 * ct, 3 * CT)
                        product(dst, sh, ml, 3 * ct + 1, 3 * CT)
                        last = product(dst, sl, mh, 3 * ct + 2, 3 * CT)
                last.then_inc(s_gram, 1)

            def conv(i, c, o):
                if not (isinstance(i, int) and i == 0 and c == 0):
                    pe.wait_ge(s_relu, (i * CH + c - 1) * CT + o + 1)
                slot = slice((c % RING) * CW, (c % RING + 1) * CW)
                for ct in range(CT):
                    h, l = wh[:, ct, o * P:(o + 1) * P], wl[:, ct, o * P:(o + 1) * P]
                    dst = psum[:, o, :]
                    pe.matmul(dst, h, gh[:, ct, slot], start=(ct == 0), stop=False)
                    pe.matmul(dst, h, gl[:, ct, slot], start=False, stop=False)
                    last = pe.matmul(dst, l, gh[:, ct, slot], start=False, stop=(ct == CT - 1))
                if o == CT - 1:
                    last.then_inc(s_chunk_used, 1)

            def picks(i, c):
                pe.wait_ge(s_after, i * CH + c + 1)
                if not (isinstance(i, int) and i == 0 and c == 0):
                    pe.wait_ge(s_fn, i * CH + c)
                dst = psum[0:REP, BANK_A, :].rearrange("p (u e w) -> p u e w", e=2, w=W)
                src = bq[:, :, (c % 2) * PAIRS * P:(c % 2 + 1) * PAIRS * P]\
                    .rearrange("p r (u e w) -> p r u e w", e=2, w=W)
                for e in range(2):
                    for k, role in enumerate((BEFORE, AFTER, SAME)):
                        u0 = 1 if role == BEFORE and c == 0 else 0
                        u1 = PAIRS - 1 if role == AFTER and c == CH - 1 else PAIRS
                        last = pe.matmul(dst[:, u0:u1, e, :], pick[:, role, e, :], src[:, role, u0:u1, e, :],
                                         start=(e == 0 and k == 0), stop=True, skip_group_check=True)
                last.then_inc(s_pick, 1)

            def turn_blocks(i, c):
                pe.wait_ge(s_masked, i * NB + PAIRS * (c + 1))
                if isinstance(i, int) and i == 0 and c == 0:
                    pe.wait_ge(s_vchain, STATS_CHAIN)
                else:
                    pe.wait_ge(s_root, i * CH + c)
                for t in range(PAIRS * c, min(PAIRS * (c + 1), NB - 1)):
                    last = pe.transpose(psum[:, BANK_N, (t % PAIRS) * P:(t % PAIRS + 1) * P],
                                        bq[:, BEFORE, ((t + 1) % PRING) * P:((t + 1) % PRING + 1) * P], ident)
                last.then_inc(s_turned, 1)

            def norm(i, c, last):
                pe.wait_ge(s_sq, i * CH + c + 1)
                if c == STATS_AT + 1 and not last:
                    pe.wait_ge(s_vchain, (i + 2) * STATS_CHAIN)
                pe.matmul(psum[0:REP, BANK_N, :], ssum[0:D, :], sq[0:D, :], start=True, stop=True)\
                  .then_inc(s_norm, 1)

            def tail(n, half):
                pe.wait_ge(s_t, n + 1)
                src = tpair[0:REP, half, :].rearrange("p (r w) -> p r w", w=W)
                for o in range(CT):
                    dst = psum[:, o, :].rearrange("p (r w) -> p r w", w=W)
                    for k in range(KS):
                        last = pe.matmul(dst[:, :, k::KS], wd[0:REP, k * C + o * P:k * C + (o + 1) * P],
                                         src[:, :, k::KS], start=False, stop=True, skip_group_check=True)
                    last.then_inc(s_conv, 1)

            def group_average(i):
                pe.wait_ge(s_xagg, 2 * i + 1)
                if not (isinstance(i, int) and i == 0):
                    pe.wait_ge(s_after, (i - 1) * CH + STATS_AT + 2)
                pe.matmul(psum[:, BANK_N, 0:CT], gavg, aggx[:, :, 0], start=True, stop=True).then_inc(s_gavg, 1)

            def group_spread(i):
                pe.wait_ge(s_xagg, 2 * i + 2)
                pe.matmul(psum[:, BANK_N, CT:2 * CT], gavg, gd[:, :], start=True, stop=True).then_inc(s_gavg, 1)

            def image(i, last):
                for c in range(CH):
                    nxt = (i, c + 1) if c + 1 < CH else None if last else (i + 1, 0)
                    convs = list(range(CT))
                    picks(i, c)
                    if not (isinstance(i, int) and i == 0 and c == 0):
                        tail(i * CH + c - 1, (c - 1) % 2)
                    if nxt:
                        pe.wait_ge(s_gl, (i * CH + min(c + 3, CH)) * CT if c + 1 < CH else ((i + 1) * CH + 2) * CT)
                        gram(nxt[0], PAIRS * nxt[1])
                        gram(nxt[0], PAIRS * nxt[1] + 1)
                    else:
                        conv(i, c, convs.pop(0))
                    norm(i, c, last)
                    if nxt:
                        gram(nxt[0], PAIRS * nxt[1] + 2)
                        gram(nxt[0], PAIRS * nxt[1] + 3)
                        conv(i, c, convs.pop(0))
                        turn_blocks(*nxt)
                    for n, o in enumerate(convs):
                        conv(i, c, o)
                        if c == STATS_AT and not last and n == 0:
                            group_average(i + 1)
                    if c == STATS_AT and not last:
                        group_spread(i + 1)

            pe.wait_ge(s_wsplit, 6)
            group_average(0)
            group_spread(0)
            for t in range(PAIRS):
                pe.wait_ge(s_gl, (2 if t == PAIRS - 1 else 1) * CT)
                gram(0, t)
            turn_blocks(0, 0)
            image(0, False)
            if B > 2:
                with pe.Fori(1, B - 1) as i:
                    image(i, False)
            image(B - 1, True)
            tail(B * CH - 1, (CH - 1) % 2)

            stats = ymv[:, :].rearrange("p (n s) -> p n s", s=2)
            pe.wait_ge(s_relu, B * CH * CT)
            pe.wait_ge(s_sstat, 1)
            pe.matmul(psum[:, 0, 0:NC], gavg, sm, start=True, stop=True).then_inc(s_smm, 1)
            pe.wait_ge(s_sstat, 2)
            pe.matmul(psum[:, 1, 0:NC], gavg, tmp, start=True, stop=True).then_inc(s_smm, 1)
            pe.wait_ge(s_sstat, 3)
            pe.wait_ge(s_w12, 64)
            gap = sgap.rearrange("p (b t) -> p b t", t=CT)
            for ct in range(CT):
                last = product(psum[0:HID, 2, 0:B], w1_sb[:, ct, :], gap[:, :, ct], ct, CT)
            last.then_inc(s_smm, 1)
            pe.wait_ge(s_sstat, 4)
            for ct in range(CT):
                last = pe.matmul(psum[:, 3, ct * B:(ct + 1) * B], w2_sb[0:HID, ct * P:(ct + 1) * P], hid[0:HID, :],
                                 start=True, stop=True)
            last.then_inc(s_smm, 1)
            pe.wait_ge(s_sstat, 5)
            pe.matmul(psum[:, 4, 0:NCLS * NC], before, onehot, start=True, stop=True).then_inc(s_smm, 1)
            pe.matmul(psum[:, 5, 0:NCLS * NC], ones, onehot, start=True, stop=True).then_inc(s_smm, 1)

            def place(g, u):
                pe.wait_ge(s_at, g + 1)
                for j in range(COLS):
                    last = pe.matmul(psum[:, 6, 0:NT], at_lane[:, u, j, :], at_tile[:, u, j, :],
                                     start=isinstance(g, int) and g == 0 and j == 0, stop=True, skip_group_check=True)
                last.then_inc(s_placed, 1)

            place(0, 0)
            place(1, 1)
            if NC // COLS > 2:
                with pe.Fori(1, NC // (2 * COLS)) as h:
                    for u in range(2):
                        place(h * 2 + u, u)

            def mix(t, u):
                s = u % 2
                pe.wait_ge(s_diag, t + 1)
                pe.wait_ge(s_pool, t + 1)
                cls_t = pe.value_load(cls_i[0:1, bass.ds(t, 1)], min_val=0, max_val=NCLS)
                with pe.If(cls_t < NCLS):
                    with pe.If(cls_t < 1):
                        mix_banks(t, u, s, False)
                    with pe.Else():
                        mix_banks(t, u, s, True)
                with pe.Else():
                    if not (isinstance(t, int) and t == 0):
                        pe.wait_ge(s_res, t * 8)
                    pe.sem_inc(s_mix, 8)

            def mix_banks(t, u, s, with_small):
                for b in range(8):
                    if not (isinstance(t, int) and t == 0):
                        pe.wait_ge(s_res, (t - 1) * 8 + b + 1)
                    dst = psum[:, b, :]
                    pe.matmul(dst, diag[:, s, 0, :], bufs[:, u, b * CW:(b + 1) * CW], start=True, stop=False)
                    if with_small:
                        pe.matmul(dst, diag[:, s, 1, :], small[:, s, b * ROWS:(b + 1) * ROWS, 1:W + 1],
                                  start=False, stop=False)
                    pe.matmul(dst, diag[:, s, 2, :], big[:, s, b * CW:(b + 1) * CW], start=False, stop=True)\
                      .then_inc(s_mix, 1)

            pe.wait_ge(s_sorted, 1)
            for u in range(BUFS):
                mix(u, u)
            with pe.Fori(1, NT // BUFS) as g:
                for u in range(BUFS):
                    mix(g * BUFS + u, u)


def kernel(x, L0_conv_W, L0_conv_bias, L1_conv_w1, L1_conv_b1, L1_conv_w2, L1_conv_b2):
    import concourse.bacc as _bacc
    from concourse.bass_utils import run_bass_kernel_spmd as _run

    nc = _bacc.Bacc("TRN2", target_bir_lowering=False, num_devices=1)
    ins = {
        "x": x, "wt": L0_conv_W[:, :C].T, "wturn": L0_conv_W.T[turned_rows()].reshape(D, KS * C),
        "bias": L0_conv_bias, "w1t": L1_conv_w1.T, "b1": L1_conv_b1,
        "w2t": L1_conv_w2.T, "b2": L1_conv_b2, "consts": const_arrays(),
    }
    arrays, args = {}, []
    for name, a in ins.items():
        a = np.ascontiguousarray(a)
        arrays[f"in_{name}"] = a
        args.append(nc.dram_tensor(f"in_{name}", a.shape, mybir.dt.from_np(a.dtype), kind="ExternalInput").ap())
    out = nc.dram_tensor("out", x.shape, mybir.dt.float32, kind="ExternalOutput").ap()
    build(nc, *args, out)
    r = _run(nc, [arrays], core_ids=[0])
    return r.results[0]["out"]
```
